# Optimizing a Trainium2 kernel written in Bass

```python
import numpy as np
import jax
import jax.numpy as jnp

def _softmax(x, axis=-1):
    return jax.nn.softmax(x, axis=axis)

def _gelu(x):
    return jax.nn.gelu(x, approximate=True)

def _silu(x):
    return jax.nn.silu(x)

def _sigmoid(x):
    return jax.nn.sigmoid(x)

def _layernorm(x, axis=-1, eps=1e-05):
    m = jnp.mean(x, axis=axis, keepdims=True)
    v = jnp.var(x, axis=axis, keepdims=True)
    return (x - m) / jnp.sqrt(v + eps)

def _scatter_add(tgt, idx, src, axis=0):
    return tgt.at[idx].add(src)

def _segment_sum(src, seg, n):
    return jax.ops.segment_sum(src, seg, n)
kernel_name = 'mk_pixart_resid_d1_seqx_r4_b9a11b'

def setup_inputs(seed: int=0):
    np.random.seed(seed)
    _w = jnp.asarray

    def _rec_inputs():
        import jax
        import jax.numpy as jnp
        _rk = jax.random.key(seed)
        x = 2.818e-05 + 1 * jax.random.normal(jax.random.fold_in(_rk, 1), (16, 256, 256), jnp.float32)
        _lenS = 256 - jax.random.randint(jax.random.fold_in(_rk, 7), (16,), 0, max(1, 256 // 4) + 1, jnp.int32)
        _lenS2 = 120 - jax.random.randint(jax.random.fold_in(_rk, 8), (16,), 0, max(1, 120 // 4) + 1, jnp.int32)
        _ctx_1024P = jax.random.normal(jax.random.fold_in(_rk, 11), (16, 16, 256), jnp.float32)
        _ctx_1024c = jax.random.dirichlet(jax.random.fold_in(_rk, 511), 0.3 * jnp.ones((16,), jnp.float32), (16, 120))
        _ctx_1024t = jnp.einsum('bsk,bkd->bsd', _ctx_1024c, _ctx_1024P)
        _ctx_1024t = _ctx_1024t * jax.lax.rsqrt(jnp.mean(jnp.square(_ctx_1024t)) + 1e-12) * 0.953939
        ctx_1024 = -0.000391444 + 0.999954 * (_ctx_1024t + 0.3 * jax.random.normal(jax.random.fold_in(_rk, 611), (16, 120, 256), jnp.float32))
        condB_pt = jax.random.uniform(jax.random.fold_in(_rk, 13), (16,), jnp.float32, 0.0, 226.919)
        return (x, ctx_1024, condB_pt, _lenS2)
    x, ctx_1024, condB_pt, _lenS2 = _rec_inputs()

    def _L0_xcond_setup():
        import jax, jax.numpy as jnp
        import numpy as np
        N, L, H, Q = (64, 258, 256, 64)
        WINDOW = 16.0
        DEV_POW = 128.0
        key = jax.random.key(seed)
        k1, k2, k3, k4, k5, k6 = jax.random.split(key, 6)
        encoder_outputs = jax.random.normal(k1, (N, L, H), dtype=jnp.float32)
        decoder_h_t = jax.random.normal(k2, (N, Q, H), dtype=jnp.float32)
        src_len = jax.random.randint(k3, (N,), 32, L + 1).astype(jnp.int32)
        p_t = jax.random.uniform(k4, (N,), dtype=jnp.float32) * (src_len.astype(jnp.float32) - 1.0)
        W_a = jax.random.normal(k5, (H, H), dtype=jnp.float32) * (1.0 / np.sqrt(H))
        W_c = jax.random.normal(k6, (H, 2 * H), dtype=jnp.float32) * (1.0 / np.sqrt(2 * H))
        return {'encoder_outputs': encoder_outputs, 'decoder_h_t': decoder_h_t, 'src_len': src_len, 'p_t': p_t, 'W_a': W_a, 'W_c': W_c}
    _L0_xcond_all = _L0_xcond_setup()
    _L0_xcond_in = {k: v for k, v in _L0_xcond_all.items() if k in ('W_a', 'W_c')}
    del _L0_xcond_all

    def _L0_ffn_setup():
        import jax, jax.numpy as jnp
        import numpy as np
        TOP_K = 2
        key = jax.random.key(seed)
        k1, k2, k3, k4 = jax.random.split(key, 4)
        B, T, D, H, E = (2, 512, 256, 512, 8)
        x = jax.random.normal(k1, (B, T, D), dtype=jnp.float32)
        w12 = jax.random.normal(k2, (E, 2 * H, D), dtype=jnp.float32) * D ** (-0.5)
        w3 = jax.random.normal(k3, (E, D, H), dtype=jnp.float32) * H ** (-0.5)
        gate_w = jax.random.normal(k4, (E, D), dtype=jnp.float32) * D ** (-0.5)
        return {'x': x, 'w12': w12, 'w3': w3, 'gate_w': gate_w}
    _L0_ffn_all = _L0_ffn_setup()
    _L0_ffn_in = {k: v for k, v in _L0_ffn_all.items() if k in ('w12', 'w3', 'gate_w')}
    del _L0_ffn_all
    return {'x': x, 'ctx_1024': ctx_1024, 'condB_pt': condB_pt, '_lenS2': _lenS2, 'L0_xcond_W_a': _L0_xcond_in['W_a'], 'L0_xcond_W_c': _L0_xcond_in['W_c'], 'L0_ffn_w12': _L0_ffn_in['w12'], 'L0_ffn_w3': _L0_ffn_in['w3'], 'L0_ffn_gate_w': _L0_ffn_in['gate_w']}

def reference(x, ctx_1024, condB_pt, _lenS2, L0_xcond_W_a, L0_xcond_W_c, L0_ffn_w12, L0_ffn_w3, L0_ffn_gate_w):
    import jax
    import jax.numpy as jnp

    def _L0_xcond_ref(encoder_outputs, decoder_h_t, src_len, p_t, W_a, W_c):
        import jax, jax.numpy as jnp
        import numpy as np
        N, L, H, Q = (64, 258, 256, 64)
        WINDOW = 16.0
        DEV_POW = 128.0
        n, l, h = encoder_outputs.shape
        idx = jnp.arange(l, dtype=jnp.float32)
        src_end = src_len.astype(jnp.float32)
        attn_start = jnp.maximum(p_t - WINDOW, 0.0)
        attn_end = jnp.minimum(p_t + WINDOW, src_end)
        mask = (idx[None, :] < attn_start[:, None]) | (idx[None, :] > attn_end[:, None])
        score = jnp.einsum('nqh,hk,nlk->nql', decoder_h_t, W_a, encoder_outputs)
        score = jnp.where(mask[:, None, :], -1000000000.0, score)
        align = jax.nn.softmax(score, axis=2)
        gauss = jnp.exp(-(idx[None, :] - p_t[:, None]) ** 2 / DEV_POW)
        align = align * gauss[:, None, :]
        context = jnp.einsum('nql,nlh->nqh', align, encoder_outputs)
        cat = jnp.concatenate([context, decoder_h_t], axis=2)
        return jnp.tanh(cat @ W_c.T)

    def _L0_ffn_ref(x, w12, w3, gate_w):
        import jax, jax.numpy as jnp
        import numpy as np
        TOP_K = 2
        E = gate_w.shape[0]
        H = w3.shape[-1]
        scores = jnp.einsum('btd,ed->bte', x, gate_w)
        topk_scores, topk_idx = jax.lax.top_k(scores, TOP_K)
        topk_probs = jax.nn.softmax(topk_scores, axis=-1)
        total_probs = jnp.sum(jax.nn.one_hot(topk_idx, E, dtype=topk_probs.dtype) * topk_probs[..., None], axis=-2)
        h12 = jnp.einsum('btd,ehd->bteh', x, w12)
        h1, h2 = (h12[..., :H], h12[..., H:])
        hidden = jax.nn.silu(h1) * h2
        expert_out = jnp.einsum('bteh,edh->bted', hidden, w3)
        y = jnp.sum(total_probs[..., None] * expert_out, axis=-2)
        return y
    x = x + _L0_xcond_ref(ctx_1024, _layernorm(x, axis=-1), _lenS2, condB_pt, L0_xcond_W_a, L0_xcond_W_c)
    x = x + _L0_ffn_ref(_layernorm(x, axis=-1), L0_ffn_w12, L0_ffn_w3, L0_ffn_gate_w)
    return x

_drawn_inputs = setup_inputs


def setup_inputs(seed=0):
    import zlib

    import numpy as np

    out = dict(_drawn_inputs(seed))
    spreads = {}
    factors = {}
    for name, (base, spread) in spreads.items():
        noise = np.random.default_rng([zlib.crc32(name.encode()), seed]).standard_normal(out[name].shape)
        drawn = base * np.exp(spread * noise) if base else spread * noise
        out[name] = jnp.asarray(drawn.astype(out[name].dtype))
    for name, factor in factors.items():
        out[name] = (out[name] * factor).astype(out[name].dtype)
    return out
```

```python
import concourse.bass as bass
from concourse import mybir
from contextlib import ExitStack

F32 = mybir.dt.float32
F32R = mybir.dt.float32r
BF16 = mybir.dt.bfloat16
I32 = mybir.dt.int32
ACT = mybir.ActivationFunctionType
ALU = mybir.AluOpType
AX = mybir.AxisListType
ds = bass.ds

P = 128
NB = 16
QT = 2
D = 256
DC = D // P
L = 120
NE = 8
FH = 512
FC = FH // P
TOK = NB * QT * P
WINDOW, DEV_POW, MASKED, EPS = 16.0, 128.0, 1.0e9, 1.0e-5
BIG = 3.0e38

META = D
IDCOL = META + NE
ROW = 272
CAP = TOK + P
XS_ROWS = NE * CAP + P
NBLK = 2 * TOK // P + NE - 1
TABW = 4

WE = DC * 2 * FH + FC * D
W2OFF = DC * 2 * FH
EARLY = 6
LATE = NE - EARLY
WCH = EARLY * WE // NB
LO1 = EARLY * WE
HI2 = 2 * EARLY * WE
LO2 = HI2 + LATE * WE
WALL = 2 * NE * WE

CREDIT = 4
U = 4


def done(n):
    return CREDIT + 1 + n


def freed(n, ring):
    return CREDIT + 1 + n - ring


def landed(n, u, ring):
    r = u % ring
    return (n - r) * (16 // ring) + 16


def settle(engine, sem):
    engine.sem_inc(sem, 1)


def link(engine, instruction, sem, value):
    instruction.then_inc(sem, 1)
    engine.wait_ge(sem, value)


def build(nc, x_d, ctx_d, cond_d, len_d, wa_d, wc_d, w_d, gate_d, out_d):
    xs = nc.dram_tensor("expert_rows", [XS_ROWS, ROW], F32, kind="Internal").ap()
    x_v = x_d.rearrange("(b j p) d -> p b j d", j=QT, p=P)
    out_v = out_d[0:TOK, :].rearrange("(b j p) d -> p b j d", j=QT, p=P)

    with ExitStack() as ctx:
        def sem(name):
            return ctx.enter_context(nc.semaphore(name))

        def sb(name, shape, dt=F32, stack=ctx):
            return stack.enter_context(nc.sbuf_tensor(name, shape, dt))

        def ps(name, shape, stack):
            return stack.enter_context(nc.psum_tensor(name, shape, F32))

        ident = sb("ident", [P, P])
        tail = sb("tail", [P, ROW])
        tab = sb("tab", [1, NBLK, TABW], I32)
        tailrow = sb("tailrow", [1, NE], I32)

        two = ExitStack()
        wall = sb("wall", [P, WALL], F32R, two)
        xb = sb("xb", [P, U, ROW], F32, two)
        meta = sb("meta", [P, U, NE + 1], stack=two)
        xt2 = sb("xt2", [P, 2, 2, DC, P], F32R, two)
        sil = sb("sil", [P, FH], stack=two)
        hid = sb("hid", [P, FH], stack=two)
        ht2 = sb("ht2", [P, 2, FC, P], F32R, two)
        yb = sb("yb", [P, 2, D], stack=two)

        two.close()
        one = ExitStack()
        sb("early", [P, HI2], stack=one)
        xt = sb("x", [P, U, QT, D], stack=one)
        x2 = sb("x2", [P, U, QT, D], stack=one)
        xrow = sb("xrow", [P, U, QT, ROW], stack=one)
        h = sb("h", [P, 2, QT, D], stack=one)
        hT = sb("hT", [P, 2, QT, DC, P], stack=one)
        h2T = sb("h2T", [P, QT, DC, P], stack=one)
        cx = sb("cx", [P, U, DC, L], stack=one)
        wst = sb("wst", [P, 2, WCH], stack=one)
        wa = sb("wa", [P, DC, D], stack=one)
        wc = sb("wc", [P, 2 * DC, D], stack=one)
        gw = sb("gw", [P, DC, NE], stack=one)
        bias = sb("bias", [P, L], stack=one)
        kn = sb("kn", [P, 2, DC, L], stack=one)
        vg = sb("vg", [L, 2, D], stack=one)
        tS = sb("tS", [P, QT, L], stack=one)
        ex = sb("ex", [P, QT, L], stack=one)
        en = sb("en", [P, 2, QT, L], stack=one)
        eT = sb("eT", [L, 2, QT, P], stack=one)
        th = sb("th", [P, QT, D], stack=one)
        tmin = sb("tmin", [P, QT], stack=one)
        rsum = sb("rsum", [P, QT], stack=one)
        rinv = sb("rinv", [P, QT], stack=one)
        bst = sb("bst", [P, 4, 6], stack=one)
        mv = sb("mv", [P, U, 4, 2], stack=one)
        ve = sb("ve", [P, 4], stack=one)
        rstd = sb("rstd", [P, U, 4], stack=one)
        nmr = sb("nmr", [P, QT], stack=one)
        mhalf = sb("mhalf", [P, 4], stack=one)
        gauss = sb("gauss", [L, NB], stack=one)
        gdev = sb("gdev", [L, NB], stack=one)
        cond = sb("cond", [P, NB], stack=one)
        leni = sb("leni", [P, NB], I32, one)
        lenf = sb("lenf", [P, NB], stack=one)
        first = sb("first", [P, NB], stack=one)
        last = sb("last", [P, NB], stack=one)
        lidx = sb("lidx", [P, L], stack=one)
        keep1 = sb("keep1", [P, L], stack=one)
        pcol = sb("pcol", [P, 1], stack=one)
        tri = sb("tri", [P, P], BF16, one)
        ones = sb("ones", [P, P], BF16, one)
        tokid = sb("tokid", [P, NB * QT], I32, one)
        ecap = sb("ecap", [P, NE], stack=one)
        rank8 = sb("rank8", [P, NE], stack=one)
        m12 = sb("m12", [P, 2, QT], stack=one)
        k12 = sb("k12", [P, 2, QT], stack=one)
        dm = sb("dm", [P, QT], stack=one)
        e2 = sb("e2", [P, QT], stack=one)
        den = sb("den", [P, QT], stack=one)
        p12 = sb("p12", [P, 2, QT], stack=one)
        rt = sb("rt", [P, QT, NE], stack=one)
        rk = sb("rk", [P, QT, NE], stack=one)
        oh = sb("oh", [P, 2, QT, NE], stack=one)
        occ = sb("occ", [P, QT, NE], BF16, one)
        occs = sb("occs", [P, NE], stack=one)
        acc = sb("acc", [P, NE], BF16, one)
        pe8 = sb("pe8", [P, QT, NE], stack=one)
        q8 = sb("q8", [P, 2, QT, NE], stack=one)
        idx = sb("idx", [P, U, 2, QT], I32, one)
        cnt = sb("cnt", [1, NE], stack=one)
        j128 = sb("j128", [1, TOK // P], stack=one)
        nblk = sb("nblk", [1, NE], stack=one)
        zero8 = sb("zero8", [1, NE], stack=one)
        one8 = sb("one8", [1, NE], stack=one)
        end8 = sb("end8", [1, NE], stack=one)
        skip8 = sb("skip8", [1, NE], stack=one)
        biota = sb("biota", [1, NBLK], stack=one)
        eb = sb("eb", [1, NBLK], stack=one)
        islate = sb("islate", [1, NBLK], stack=one)
        hib = sb("hib", [1, NBLK], stack=one)
        rowb = sb("rowb", [1, NBLK], stack=one)
        past = wst[0:1, 0, 0:NBLK * NE].rearrange("a (b e) -> a b e", e=NE)
        prod = wst[0:1, 0, NBLK * NE:2 * NBLK * NE].rearrange("a (b e) -> a b e", e=NE)
        gt = wst[0:1, 1, 0:NE * (TOK // P)].rearrange("a (e j) -> a e j", e=NE)
        one.close()
        braw = ExitStack()
        sb("fence", [P, LO2], F32, braw)
        wraw = sb("wraw", [P, LATE * WE], F32, braw)
        braw.close()

        p1 = ExitStack()
        psK = ps("psK", [P, DC, 256], p1)
        psV = ps("psV", [P, 512], p1)
        psHT = ps("psHT", [P, QT, DC, P], p1)
        psS = ps("psS", [P, QT, 256], p1)
        psET = ps("psET", [P, QT, 256], p1)
        psO = ps("psO", [P, QT, D], p1)
        psH2T = ps("psH2T", [P, QT, DC, P], p1)
        psR = ps("psR", [P, 4, P], p1)
        p1.close()
        psX = ps("psX", [P, 4, P], p1)
        psHH = ps("psHH", [P, FC, P], p1)
        psH1 = ps("psH1", [P, FH], p1)
        psH2 = ps("psH2", [P, FH], p1)
        psY = ps("psY", [P, 2, 512], p1)
        p1.close()
        score = psR[:, 0, 0:QT * NE].rearrange("p (j e) -> p j e", e=NE)
        pos = psR[:, 1, 0:QT * NE].rearrange("p (j e) -> p j e", e=NE)
        total = psR[:, 2, 0:NE]

        s_small = sem("s_small")
        s_x = [sem(f"s_xin{i}") for i in range(U)]
        s_cx = [sem(f"s_cx{i}") for i in range(U)]
        s_w = [sem(f"s_win{i}") for i in range(2)]
        s_x2out = [sem(f"s_x2out{i}") for i in range(U)]
        s_fill = sem("s_fill")
        s_scat = sem("s_scat")
        s_rows = sem("s_rows")
        s_late = sem("s_late")
        s_xb = [sem(f"s_xb{i}") for i in range(U)]
        s_add = sem("s_add")
        s_settle_pool = sem("s_settle_pool")
        s_settle_dve = sem("s_settle_dve")
        s_iota = sem("s_iota")
        s_cst = sem("s_cst")
        s_mask = sem("s_mask")
        s_gdev = sem("s_gdev")
        s_gauss = sem("s_gauss")
        s_kv = sem("s_kv")
        s_kn = sem("s_kn")
        s_vg = sem("s_vg")
        s_st = sem("s_st")
        s_st2 = sem("s_st2")
        s_ve = sem("s_ve")
        s_rstd = sem("s_rstd")
        s_h = sem("s_h")
        s_hTp = sem("s_hTp")
        s_hT = sem("s_hT")
        s_s = sem("s_s")
        s_t = sem("s_t")
        s_ex = sem("s_ex")
        s_en = sem("s_en")
        s_sm = sem("s_sm")
        s_eTp = sem("s_eTp")
        s_eT = sem("s_eT")
        s_o = sem("s_o")
        s_th = sem("s_th")
        s_x2 = sem("s_x2")
        s_nmr = sem("s_nmr")
        s_h2 = sem("s_h2")
        s_h2Tp = sem("s_h2Tp")
        s_h2T = sem("s_h2T")
        s_g = sem("s_g")
        s_r1 = sem("s_r1")
        s_occ = sem("s_occ")
        s_e2 = sem("s_e2")
        s_rp = sem("s_rp")
        s_p = sem("s_p")
        s_r2 = sem("s_r2")
        s_pe = sem("s_pe")
        s_idx = sem("s_idx")
        s_acc = sem("s_acc")
        s_whi = sem("s_whi")
        s_wlo = sem("s_wlo")
        s_tot = sem("s_tot")
        s_tc = sem("s_tc")
        s_tailrow = sem("s_tailrow")
        s_tab = sem("s_tab")
        s_late_hi = sem("s_late_hi")
        s_late_lo = sem("s_late_lo")
        s_xtp = sem("s_xtp")
        s_meta = sem("s_meta")
        s_xhi = sem("s_xhi")
        s_xlo = sem("s_xlo")
        s_h1 = sem("s_h1")
        s_hh = sem("s_hh")
        s_sil = sem("s_sil")
        s_hid = sem("s_hid")
        s_htp = sem("s_htp")
        s_hhi = sem("s_hhi")
        s_hlo = sem("s_hlo")
        s_y = sem("s_y")
        s_yb = sem("s_yb")

        block = ctx.enter_context(nc.Block())

        def start(engine, *sems):
            for s in sems:
                engine.sem_inc(s, CREDIT)

        def here(n):
            return not isinstance(n, int) or 0 <= n < NB

        def phase1(engine, step, stages=5):
            for s in range(U):
                step(s, s)
            with engine.Fori(U, NB - U + 1, U) as g:
                for u in range(U):
                    step(g + u, u)
            for s in range(NB, NB + stages - 1):
                step(s, s % U)

        def in_blocks(n):
            return not isinstance(n, int) or 0 <= n < NBLK

        LOOP2 = (NBLK - 2) // U * U

        def phase2(engine, step):
            for i in range(2):
                step(i, i % U)
            with engine.Fori(2, 2 + LOOP2 - U + 1, U) as g:
                for u in range(U):
                    step(g + u, (2 + u) % U)
            for i in range(2 + LOOP2, NBLK + 2):
                step(i, i % U)

        @block.sync
        def _(sp):
            sp.dma_start(cond[:, :], cond_d.rearrange("(a n) -> a n", a=1).to_broadcast([P, NB])).then_inc(s_small, 16)
            sp.dma_start(leni[:, :], len_d.rearrange("(a n) -> a n", a=1).to_broadcast([P, NB])).then_inc(s_small, 16)
            sp.dma_start(wa[:, :, :], wa_d).then_inc(s_small, 16)
            sp.dma_start(wc[:, :, :], wc_d).then_inc(s_small, 16)
            sp.dma_start(gw[:, :, :], gate_d).then_inc(s_small, 16)

            def load(b, u):
                sp.wait_ge(s_x2, freed(b, U))
                sp.dma_start(xt[:, u, :, :], x_v[:, ds(b, 1), :, :].rearrange("p b j d -> p (b j) d")).then_inc(s_x[u], 16)
                sp.wait_ge(s_kv, freed(b, U))
                sp.dma_start(cx[:, u, :, :], ctx_d[:, ds(b, 1), :, :].rearrange("p b c l -> p (b c) l")).then_inc(s_cx[u], 16)
                sp.wait_ge(s_wlo, freed(b, 2))
                sp.dma_start(wst[:, u % 2, :], w_d[:, ds(b * WCH, WCH)]).then_inc(s_w[u % 2], 16)

            def store(b, u):
                sp.wait_ge(s_x2, done(b))
                sp.dma_start(out_v[:, ds(b, 1), :, :].rearrange("p b j d -> p (b j) d"), x2[:, u, :, :]).then_inc(s_x2out[u], 16)

            for u in range(U):
                sp.sem_inc(s_x2out[u], 16)
            for t in range(U):
                load(t, t)
            store(0, 0)
            with sp.Fori(U, NB - U + 1, U) as g:
                for u in range(U):
                    load(g + u, u)
                    store(g + (u - 3), (u + 1) % U)
            for b in range(NB - 3, NB):
                store(b, b % U)

            sp.wait_ge(s_cst, 1)
            sp.dma_start(xs[NE * CAP:NE * CAP + P, :], tail[:, :]).then_inc(s_fill, 16)
            sp.dma_start(out_d[TOK:TOK + P, :], tail[:, 0:D]).then_inc(s_fill, 16)
            sp.wait_ge(s_scat, 64 * NB)
            for u in range(U):
                sp.wait_ge(s_x2out[u], 16 * (NB // U) + 16)
            sp.wait_ge(s_tailrow, 1)
            for e in range(NE):
                r = sp.value_load(tailrow[0:1, e:e + 1], min_val=e * CAP, max_val=e * CAP + TOK)
                sp.dma_start(xs[ds(r, P), :], tail[:, :]).then_inc(s_fill, 16)
            sp.wait_ge(s_tab, 1)
            sp.wait_ge(s_wlo, done(NB - 1))
            sp.wait_ge(s_fill, 16 * (NE + 2))

            def load_block(b, u):
                r = sp.value_load(tab[0:1, ds(b, 1), 0:1].rearrange("a b c -> a (b c)"), min_val=0, max_val=NE * CAP)
                sp.wait_ge(s_xtp, freed(b, U))
                sp.wait_ge(s_meta, freed(b, U))
                sp.dma_start(xb[:, u, :], xs[ds(r, P), :]).then_inc(s_xb[u], 16)

            load_block(0, 0)
            load_block(1, 1)
            sp.dma_start(wraw[:, :], w_d[:, EARLY * WE:NE * WE]).then_inc(s_late, 16)
            load_block(2, 2)
            load_block(3, 3)
            with sp.Fori(U, NBLK // U * U - U + 1, U) as g:
                for u in range(U):
                    load_block(g + u, u)
            for b in range(NBLK // U * U, NBLK):
                load_block(b, b % U)
            sp.wait_ge(s_add, 16 * NBLK)

        @block.gpsimd
        def _(pool):
            start(pool, s_x2, s_rstd, s_rows)
            n = 0

            def made(instruction):
                nonlocal n
                n += 1
                link(pool, instruction, s_iota, n)

            exact = dict(allow_small_or_imprecise_dtypes=True)
            made(pool.memset(ident[:, :], 0.0))
            made(pool.affine_select(out=ident[:, :], in_=ident[:, :], compare_op=ALU.not_equal, fill=1.0,
                                    base=0, pattern=[[-1, P]], channel_multiplier=1))
            made(pool.memset(ones[:, :], 1.0))
            made(pool.memset(mhalf[:, :], -0.5))
            made(pool.affine_select(out=tri[:, :], in_=ones[:, :], compare_op=ALU.is_gt, fill=0.0,
                                    base=0, pattern=[[1, P]], channel_multiplier=-1))
            made(pool.iota(lidx[:, :], pattern=[[1, L]], base=0, channel_multiplier=0, **exact))
            made(pool.iota(pcol[:, :], pattern=[[0, 1]], base=0, channel_multiplier=1, **exact))
            made(pool.iota(tokid[:, :], pattern=[[P, NB * QT]], base=0, channel_multiplier=1))
            made(pool.iota(ecap[:, :], pattern=[[CAP, NE]], base=0, channel_multiplier=0, **exact))
            made(pool.iota(rank8[:, :], pattern=[[-1, NE]], base=NE, channel_multiplier=0, **exact))
            made(pool.iota(j128[:, :], pattern=[[P, TOK // P]], base=0, channel_multiplier=0, **exact))
            made(pool.iota(biota[:, :], pattern=[[1, NBLK]], base=0, channel_multiplier=0, **exact))
            made(pool.memset(zero8[:, :], 0.0))
            made(pool.memset(one8[:, :], 1.0))
            made(pool.memset(tail[:, :], 0.0))
            made(pool.memset(acc[:, :], 0.0))
            made(pool.memset(xrow[:, :, :, META:ROW], 0.0))
            pool.iota(tail[:, IDCOL:IDCOL + 1].bitcast(I32), pattern=[[0, 1]], base=TOK, channel_multiplier=1).then_inc(s_cst, 1)

            def scatter(b, u, k, j):
                pool.indirect_dma_start(xs, bass.IndirectOffsetOnAxis(ap=idx[:, u, k, j:j + 1], axis=0),
                                        xrow[:, u, j, :], None).then_inc(s_scat, 16)

            def step(s, u):
                o, uo = s - 2, (u - 2) % U
                r, ur = s - 4, u
                if here(r):
                    pool.wait_ge(s_idx, done(r))
                    settle(pool, s_settle_pool)
                    scatter(r, ur, 0, 0)
                    scatter(r, ur, 1, 0)
                    scatter(r, ur, 0, 1)
                if here(o):
                    pool.wait_ge(s_x2out[uo], 4 * (o - uo) + 16)
                    pool.wait_ge(s_h2, freed(o, U))
                    pool.wait_ge(s_th, done(o))
                    pool.tensor_tensor(x2[:, uo, :, :], xt[:, uo, :, :], th[:, :, :], ALU.add).then_inc(s_x2, 1)
                lo, hi = (0 if here(s) else 2), (4 if here(o) else 2)
                if lo < hi:
                    pool.wait_ge(s_ve, done(s))
                    pool.tensor_tensor(rstd[:, u, lo:hi], ve[:, lo:hi], mhalf[:, lo:hi], ALU.pow).then_inc(s_rstd, 1)
                if here(r):
                    pool.wait_ge(s_scat, 64 * r + 48)
                    pool.sem_inc(s_rows, 1)
                    scatter(r, ur, 1, 1)

            phase1(pool, step)

            pool.wait_ge(s_fill, 16 * (NE + 2))
            for u in range(U):
                pool.wait_ge(s_x2out[u], 16 * (NB // U) + 16)

            def step2(i, u):
                k, uk = i - 2, (u - 2) % U
                if in_blocks(k):
                    pool.wait_ge(s_yb, done(k))
                    if not isinstance(k, int) or k > 0:
                        pool.wait_ge(s_add, 16 * k)
                    settle(pool, s_settle_pool)
                    pool.indirect_dma_start(out_d, bass.IndirectOffsetOnAxis(ap=meta[:, uk, NE:NE + 1].bitcast(I32), axis=0),
                                            yb[:, uk % 2, :], None, compute_op=ALU.add).then_inc(s_add, 16)

            for i in range(3):
                step2(i, i % U)
            with pool.Fori(3, 3 + LOOP2 - U + 1, U) as g:
                for u in range(U):
                    step2(g + u, (3 + u) % U)
            for i in range(3 + LOOP2, NBLK + 2):
                step2(i, i % U)

        @block.scalar
        def _(act):
            start(act, s_vg, s_eT, s_hT, s_h2T, s_e2, s_whi, s_th, s_ex, s_h2, s_xhi, s_hhi, s_sil, s_yb)
            act.wait_ge(s_gdev, 2)
            act.activation(gauss[:, :], gdev[:, :], ACT.Exp, scale=-1.0 / DEV_POW).then_inc(s_gauss, 1)
            act.wait_ge(s_gauss, 1)

            def step(s, u):
                a, ua = s - 1, (u - 1) % U
                o, uo = s - 2, (u - 2) % U
                h_, uh = s - 3, (u - 3) % U
                r = s - 4
                if here(a):
                    act.wait_ge(s_kv, done(a))
                    act.wait_ge(s_o, freed(a, 2))
                    act.activation(vg[:, ua % 2, :], psV[0:L, 0:D], ACT.Copy,
                                   scale=gauss[:, ds(a, 1)]).then_inc(s_vg, 1)
                if here(o):
                    act.wait_ge(s_eTp, done(o))
                    act.wait_ge(s_o, freed(o, 2))
                    act.activation(eT[:, uo % 2, :, :], psET[0:L, :, 0:P], ACT.Copy).then_inc(s_eT, 1)
                if here(a):
                    act.wait_ge(s_hTp, done(a))
                    act.activation(hT[:, ua % 2, :, :, :], psHT[:, :, :, :], ACT.Copy).then_inc(s_hT, 1)
                if here(h_):
                    act.wait_ge(s_h2Tp, done(h_))
                    act.wait_ge(s_g, freed(h_, 1))
                    act.activation(h2T[:, :, :, :], psH2T[:, :, :, :], ACT.Copy).then_inc(s_h2T, 1)
                if here(r):
                    act.wait_ge(s_rp, 4 * r + 1)
                    act.activation(e2[:, :], dm[:, :], ACT.Exp).then_inc(s_e2, 1)
                if here(s):
                    act.wait_ge(s_w[u % 2], landed(s, u, 2))
                    act.activation(wall[:, ds(s * WCH, WCH)], wst[:, u % 2, :], ACT.Copy).then_inc(s_whi, 1)
                if here(o):
                    act.wait_ge(s_o, done(o))
                    act.wait_ge(s_x2, freed(o, 1))
                    act.activation(th[:, :, :], psO[:, :, :], ACT.Tanh).then_inc(s_th, 1)
                if here(a):
                    act.wait_ge(s_t, done(a))
                    act.wait_ge(s_en, freed(a, 1))
                    act.activation(ex[:, 0, :], tS[:, 0, :], ACT.Exp, bias=tmin[:, 0:1], scale=-1.0,
                                   accum_out=rsum[:, 0:1])
                    act.activation(ex[:, 1, :], tS[:, 1, :], ACT.Exp, bias=tmin[:, 1:2], scale=-1.0,
                                   accum_out=rsum[:, 1:2]).then_inc(s_ex, 1)
                if here(o):
                    act.wait_ge(s_nmr, done(o))
                    act.wait_ge(s_rows, freed(o, U - 1))
                    act.wait_ge(s_h2Tp, freed(o, U))
                    act.activation(xrow[:, uo, 0, 0:D], x2[:, uo, 0, :], ACT.Identity,
                                   bias=nmr[:, 0:1], scale=rstd[:, u, 2:3])
                    act.activation(xrow[:, uo, 1, 0:D], x2[:, uo, 1, :], ACT.Identity,
                                   bias=nmr[:, 1:2], scale=rstd[:, u, 3:4]).then_inc(s_h2, 1)

            phase1(act, step)

            act.wait_ge(s_late, 16)
            for e in range(LATE):
                act.activation(wall[:, HI2 + e * WE:HI2 + (e + 1) * WE], wraw[:, e * WE:(e + 1) * WE],
                               ACT.Copy).then_inc(s_late_hi, 1)

            def step2(i, u):
                j = i - 1
                k, uk = i - 2, (u - 2) % U
                if in_blocks(i):
                    act.wait_ge(s_xtp, done(i))
                    act.wait_ge(s_hh, freed(i, 2))
                    act.activation(xt2[:, u % 2, 0, :, :], psX[:, 0:DC, :], ACT.Copy).then_inc(s_xhi, 1)
                if in_blocks(k):
                    act.wait_ge(s_htp, done(k))
                    act.wait_ge(s_y, freed(k, 1))
                    act.activation(ht2[:, 0, :, :], psHH[:, :, :], ACT.Copy).then_inc(s_hhi, 1)
                if in_blocks(j):
                    act.wait_ge(s_h1, done(j))
                    act.wait_ge(s_hid, freed(j, 1))
                    act.activation(sil[:, :], psH1[:, :], ACT.Silu).then_inc(s_sil, 1)
                if in_blocks(k):
                    e = act.value_load(tab[0:1, ds(k, 1), 3:4].rearrange("a b c -> a (b c)"), min_val=0, max_val=NE - 1)
                    act.wait_ge(s_y, done(k))
                    if not isinstance(k, int) or k > 1:
                        act.wait_ge(s_add, 16 * (k - 1))
                    act.activation(yb[:, uk % 2, :], psY[:, uk % 2, 0:D], ACT.Copy,
                                   scale=meta[:, uk, ds(e, 1)]).then_inc(s_yb, 1)

            for i in range(4):
                step2(i, i % U)
            with act.Fori(4, LOOP2 + 4 - U - U + 1, U) as g:
                for u in range(U):
                    step2(g + u, u)
            for i in range(LOOP2 + 4 - U, NBLK + 2):
                step2(i, i % U)

        @block.vector
        def _(dve):
            start(dve, s_kn, s_ve, s_h, s_t, s_en, s_nmr, s_occ, s_pe, s_idx, s_acc, s_wlo,
                  s_meta, s_xlo, s_hid, s_hlo)
            n = 0

            def made(instruction):
                nonlocal n
                n += 1
                link(dve, instruction, s_mask, n)

            dve.wait_ge(s_small, 80)
            dve.wait_ge(s_cst, 1)
            made(dve.tensor_copy(lenf[:, :], leni[:, :]))
            made(dve.tensor_scalar(first[:, :], cond[:, :], -WINDOW, 0.0, ALU.add, ALU.max))
            made(dve.tensor_scalar(last[:, :], cond[:, :], WINDOW, None, ALU.add))
            made(dve.tensor_tensor(last[:, :], last[:, :], lenf[:, :], ALU.min))
            dve.tensor_scalar(gdev[:, :], cond[0:L, :], pcol[0:L, 0:1], None, ALU.subtract).then_inc(s_gdev, 1)
            dve.wait_ge(s_gdev, 1)
            dve.tensor_tensor(gdev[:, :], gdev[:, :], gdev[:, :], ALU.mult).then_inc(s_gdev, 1)

            def step(s, u):
                a, ua = s - 1, (u - 1) % U
                o, uo = s - 2, (u - 2) % U
                r = s - 4
                R1, RP, R2 = 10, 4, 5
                if here(r):
                    d8 = rank8[:, :].unsqueeze(1).to_broadcast([P, QT, NE])

                    def wide(v):
                        return v.unsqueeze(2).to_broadcast([P, QT, NE])

                    def l1(instruction, q):
                        link(dve, instruction, s_r1, R1 * r + q)

                    dve.wait_ge(s_g, done(r))
                    l1(dve.tensor_reduce(m12[:, 0, :], score, AX.X, ALU.max), 1)
                    l1(dve.tensor_tensor(rt[:, :, :], score, wide(m12[:, 0, :]), ALU.is_equal), 2)
                    l1(dve.tensor_tensor(rk[:, :, :], rt[:, :, :], d8, ALU.mult), 3)
                    l1(dve.tensor_reduce(k12[:, 0, :], rk[:, :, :], AX.X, ALU.max), 4)
                    l1(dve.tensor_tensor(oh[:, 0, :, :], d8, wide(k12[:, 0, :]), ALU.is_equal), 5)
                    l1(dve.scalar_tensor_tensor(out=rt[:, :, :], in0=oh[:, 0, :, :], scalar=-BIG, in1=score,
                                                op0=ALU.mult, op1=ALU.add), 6)
                    l1(dve.tensor_reduce(m12[:, 1, :], rt[:, :, :], AX.X, ALU.max), 7)
                    dve.wait_ge(s_e2, freed(r, 1))
                    dve.tensor_tensor(dm[:, :], m12[:, 1, :], m12[:, 0, :], ALU.subtract).then_inc(s_rp, 1)
                    l1(dve.tensor_tensor(rk[:, :, :], rt[:, :, :], wide(m12[:, 1, :]), ALU.is_equal), 8)
                    l1(dve.tensor_tensor(rt[:, :, :], rk[:, :, :], d8, ALU.mult), 9)
                    l1(dve.tensor_reduce(k12[:, 1, :], rt[:, :, :], AX.X, ALU.max), 10)
                    dve.tensor_tensor(oh[:, 1, :, :], d8, wide(k12[:, 1, :]), ALU.is_equal).then_inc(s_r2, 1)
                    dve.wait_ge(s_r2, R2 * r + 1)
                    dve.wait_ge(s_p, freed(r, 1))
                    dve.tensor_tensor(occ[:, :, :], oh[:, 0, :, :], oh[:, 1, :, :], ALU.add).then_inc(s_occ, 1)
                if here(a):
                    dve.wait_ge(s_rstd, done(s - 1))
                    dve.wait_ge(s_hTp, freed(a, 2))
                    for j in range(QT):
                        last_h = dve.tensor_scalar(h[:, ua % 2, j, :], xt[:, ua, j, :], mv[:, ua, j, 0:1],
                                                   rstd[:, ua, j:j + 1], ALU.subtract, ALU.mult)
                    last_h.then_inc(s_h, 1)
                if here(r):
                    dve.wait_ge(s_e2, done(r))
                    link(dve, dve.tensor_scalar(den[:, :], e2[:, :], 1.0, None, ALU.add), s_rp, RP * r + 2)
                    link(dve, dve.reciprocal(p12[:, 0, :], den[:, :]), s_rp, RP * r + 3)
                    link(dve, dve.tensor_tensor(p12[:, 1, :], e2[:, :], p12[:, 0, :], ALU.mult), s_rp, RP * r + 4)
                    dve.tensor_tensor(rt[:, :, :], oh[:, 0, :, :], wide(p12[:, 0, :]), ALU.mult).then_inc(s_r2, 1)
                    dve.tensor_tensor(rk[:, :, :], oh[:, 1, :, :], wide(p12[:, 1, :]), ALU.mult).then_inc(s_r2, 1)
                    dve.wait_ge(s_r2, R2 * r + 3)
                    dve.tensor_tensor(xrow[:, u, :, META:META + NE], rt[:, :, :], rk[:, :, :], ALU.add)
                    dve.tensor_copy(xrow[:, u, :, IDCOL:IDCOL + 1].bitcast(I32),
                                    tokid[:, ds(QT * r, QT)].unsqueeze(2))
                if here(a):
                    dve.tensor_scalar(keep1[:, :], lidx[:, :], first[:, ds(a, 1)], -1.0, ALU.is_ge, ALU.mult).then_inc(s_sm, 1)
                    dve.wait_ge(s_sm, 4 * a + 1)
                    dve.scalar_tensor_tensor(out=keep1[:, :], in0=lidx[:, :], scalar=last[:, ds(a, 1)], in1=keep1[:, :],
                                             op0=ALU.is_le, op1=ALU.mult).then_inc(s_sm, 1)
                    dve.wait_ge(s_sm, 4 * a + 2)
                    dve.tensor_scalar(bias[:, :], keep1[:, :], MASKED, MASKED, ALU.mult, ALU.add).then_inc(s_sm, 1)
                    dve.wait_ge(s_kv, done(a))
                    dve.wait_ge(s_s, freed(a, 2))
                    dve.tensor_tensor(kn[:, ua % 2, :, :], psK[:, :, 0:L],
                                      keep1[:, :].unsqueeze(1).to_broadcast([P, DC, L]), ALU.mult).then_inc(s_kn, 1)
                if here(r):
                    dve.wait_ge(s_p, done(r))
                    dve.tensor_tensor(pe8[:, :, :], pos, ecap[:, :].unsqueeze(1).to_broadcast([P, QT, NE]),
                                      ALU.add).then_inc(s_pe, 1)
                    dve.wait_ge(s_pe, done(r))
                    dve.tensor_tensor(q8[:, :, :, :], oh[:, :, :, :],
                                      pe8[:, :, :].unsqueeze(1).to_broadcast([P, 2, QT, NE]), ALU.mult).then_inc(s_r2, 1)
                    dve.wait_ge(s_r2, R2 * r + 4)
                    with nc.allow_low_precision(reason="sums of whole numbers below 2**24 are exact"):
                        dve.tensor_reduce(idx[:, u, :, :], q8[:, :, :, :], AX.X, ALU.add).then_inc(s_idx, 1)
                    dve.tensor_tensor(occs[:, :], occ[:, 0, :], occ[:, 1, :], ALU.add).then_inc(s_r2, 1)
                    dve.wait_ge(s_r2, R2 * r + 5)
                    dve.tensor_tensor(acc[:, :], acc[:, :], occs[:, :], ALU.add).then_inc(s_acc, 1)
                if here(s):
                    dve.wait_ge(s_x[u], landed(s, u, U))
                    dve.bn_stats(bst[:, 0, :], xt[:, u, 0, :]).then_inc(s_st, 1)
                    dve.bn_stats(bst[:, 1, :], xt[:, u, 1, :]).then_inc(s_st, 1)
                    dve.wait_ge(s_st, 4 * s + 2)
                    dve.wait_ge(s_whi, done(s))
                    dve.tensor_tensor(wall[:, ds(LO1 + s * WCH, WCH)], wst[:, u % 2, :],
                                      wall[:, ds(s * WCH, WCH)].bitcast(F32), ALU.subtract).then_inc(s_wlo, 1)
                    dve.bn_aggr(mv[:, u, 0, :], bst[:, 0, :]).then_inc(s_st, 1)
                    dve.bn_aggr(mv[:, u, 1, :], bst[:, 1, :]).then_inc(s_st, 1)
                if here(a):
                    dve.wait_ge(s_s, done(a))
                    dve.wait_ge(s_ex, freed(a, 1))
                    dve.wait_ge(s_sm, 4 * a + 3)
                    settle(dve, s_settle_dve)
                    for j in range(QT):
                        last_t = dve.tensor_tensor_reduce(out=tS[:, j, :], in0=psS[:, j, 0:L], in1=bias[:, :],
                                                          scale=1.0, scalar=BIG, op0=ALU.add, op1=ALU.min,
                                                          accum_out=tmin[:, j:j + 1])
                    last_t.then_inc(s_t, 1)
                    dve.wait_ge(s_ex, done(a))
                    dve.reciprocal(rinv[:, :], rsum[:, :]).then_inc(s_sm, 1)
                    dve.wait_ge(s_sm, 4 * a + 4)
                    dve.wait_ge(s_eTp, freed(a, 2))
                    dve.tensor_tensor(en[:, ua % 2, :, :], ex[:, :, :],
                                      rinv[:, :].unsqueeze(2).to_broadcast([P, QT, L]), ALU.mult).then_inc(s_en, 1)
                if here(o):
                    dve.wait_ge(s_x2, done(o))
                    dve.bn_stats(bst[:, 2, :], x2[:, uo, 0, :]).then_inc(s_st2, 1)
                    dve.bn_stats(bst[:, 3, :], x2[:, uo, 1, :]).then_inc(s_st2, 1)
                    dve.wait_ge(s_st2, 4 * o + 2)
                    settle(dve, s_settle_dve)
                    dve.bn_aggr(mv[:, u, 2, :], bst[:, 2, :]).then_inc(s_st2, 1)
                    dve.bn_aggr(mv[:, u, 3, :], bst[:, 3, :]).then_inc(s_st2, 1)
                    dve.wait_ge(s_st2, 4 * o + 4)
                lo, hi = (0 if here(s) else 2), (4 if here(o) else 2)
                if lo < hi:
                    if here(s):
                        dve.wait_ge(s_st, 4 * s + 4)
                    dve.wait_ge(s_rstd, done(s - 1))
                    dve.tensor_scalar(ve[:, lo:hi], mv[:, u, lo:hi, 1:2].rearrange("p a b -> p (a b)"), EPS, None, ALU.add).then_inc(s_ve, 1)
                if here(o):
                    dve.wait_ge(s_rstd, done(s))
                    dve.wait_ge(s_h2, freed(o, 1))
                    dve.scalar_tensor_tensor(out=nmr[:, :], in0=mv[:, u, 2:4, 0:1].rearrange("p a b -> p (a b)"), scalar=-1.0,
                                             in1=rstd[:, u, 2:4], op0=ALU.mult, op1=ALU.mult).then_inc(s_nmr, 1)

            phase1(dve, step)

            q = 0

            def t(instruction):
                nonlocal q
                q += 1
                link(dve, instruction, s_tc, q)

            dve.wait_ge(s_tot, 1)
            t(dve.tensor_copy(cnt[:, :], total[0:1, :]))
            dve.tensor_tensor(tailrow[:, :], cnt[:, :], ecap[0:1, :], ALU.add).then_inc(s_tailrow, 1)
            NJ = TOK // P
            t(dve.tensor_tensor(gt[:, :, :], cnt[:, :].unsqueeze(2).to_broadcast([1, NE, NJ]),
                                j128[:, :].unsqueeze(1).to_broadcast([1, NE, NJ]), ALU.is_gt))
            t(dve.tensor_reduce(nblk[:, :], gt[:, :, :], AX.X, ALU.add))
            t(dve.tensor_tensor_scan(end8[:, :], one8[:, :], nblk[:, :], initial=0.0, op0=ALU.mult, op1=ALU.add))
            t(dve.tensor_scalar(skip8[:, :], nblk[:, :], -float(P), float(CAP), ALU.mult, ALU.add))
            t(dve.tensor_tensor(past[:, :, :], biota[:, :].unsqueeze(2).to_broadcast([1, NBLK, NE]),
                                end8[:, :].unsqueeze(1).to_broadcast([1, NBLK, NE]), ALU.is_ge))
            t(dve.tensor_reduce(eb[:, :], past[:, :, :], AX.X, ALU.add))
            t(dve.tensor_tensor(prod[:, :, :], past[:, :, :],
                                skip8[:, :].unsqueeze(1).to_broadcast([1, NBLK, NE]), ALU.mult))
            t(dve.tensor_reduce(rowb[:, :], prod[:, :, :], AX.X, ALU.add))
            t(dve.scalar_tensor_tensor(out=rowb[:, :], in0=biota[:, :], scalar=float(P), in1=rowb[:, :],
                                       op0=ALU.mult, op1=ALU.add))

            def column(c):
                return tab[:, :, c:c + 1].rearrange("a b c -> a (b c)")

            t(dve.tensor_scalar(column(0), rowb[:, :], float(NE * CAP), None, ALU.min))
            t(dve.tensor_scalar(eb[:, :], eb[:, :], float(NE - 1), None, ALU.min))
            t(dve.tensor_copy(column(3), eb[:, :]))
            t(dve.tensor_scalar(islate[:, :], eb[:, :], float(EARLY), None, ALU.is_ge))
            t(dve.tensor_scalar(eb[:, :], eb[:, :], float(WE), None, ALU.mult))
            t(dve.scalar_tensor_tensor(out=hib[:, :], in0=islate[:, :], scalar=float(LO1), in1=eb[:, :],
                                       op0=ALU.mult, op1=ALU.add))
            t(dve.tensor_copy(column(1), hib[:, :]))
            t(dve.tensor_scalar(islate[:, :], islate[:, :], float(LATE * WE - LO1), float(LO1), ALU.mult, ALU.add))
            dve.tensor_tensor(column(2), hib[:, :], islate[:, :], ALU.add).then_inc(s_tab, 1)

            for e in range(LATE):
                dve.wait_ge(s_late_hi, e + 1)
                dve.tensor_tensor(wall[:, LO2 + e * WE:LO2 + (e + 1) * WE], wraw[:, e * WE:(e + 1) * WE],
                                  wall[:, HI2 + e * WE:HI2 + (e + 1) * WE].bitcast(F32), ALU.subtract).then_inc(s_late_lo, 1)

            def step2(i, u):
                j, k = i - 1, i - 2
                if in_blocks(i):
                    dve.wait_ge(s_xb[u], landed(i, u, U))
                    if not isinstance(i, int) or i >= U:
                        dve.wait_ge(s_add, 16 * (i - U + 1))
                    dve.tensor_copy(meta[:, u, :], xb[:, u, META:IDCOL + 1]).then_inc(s_meta, 1)
                    dve.wait_ge(s_xhi, done(i))
                    dve.tensor_tensor(xt2[:, u % 2, 1, :, :], psX[:, 0:DC, :], xt2[:, u % 2, 0, :, :].bitcast(F32),
                                      ALU.subtract).then_inc(s_xlo, 1)
                if in_blocks(k):
                    dve.wait_ge(s_hhi, done(k))
                    dve.tensor_tensor(ht2[:, 1, :, :], psHH[:, :, :], ht2[:, 0, :, :].bitcast(F32),
                                      ALU.subtract).then_inc(s_hlo, 1)
                if in_blocks(j):
                    dve.wait_ge(s_sil, done(j))
                    dve.wait_ge(s_hh, done(j))
                    dve.wait_ge(s_htp, freed(j, 1))
                    dve.tensor_tensor(hid[:, :], sil[:, :], psH2[:, :], ALU.mult).then_inc(s_hid, 1)

            for i in range(4):
                step2(i, i % U)
            with dve.Fori(4, LOOP2 + 4 - U - U + 1, U) as g:
                for u in range(U):
                    step2(g + u, u)
            for i in range(LOOP2 + 4 - U, NBLK + 2):
                step2(i, i % U)

        @block.tensor
        def _(pe):
            start(pe, s_kv, s_eTp, s_hTp, s_h2Tp, s_o, s_p, s_s, s_g, s_xtp, s_htp, s_h1, s_hh, s_y)
            pe.wait_ge(s_small, 80)
            pe.wait_ge(s_cst, 1)
            pe.wait_ge(s_gauss, 1)

            def step(s, u):
                a, ua = s - 1, (u - 1) % U
                o, uo = s - 2, (u - 2) % U
                h_, uh = s - 3, (u - 3) % U
                r = s - 4
                if here(a):
                    pe.wait_ge(s_cx[ua], landed(a, ua, U))
                    pe.wait_ge(s_kn, freed(a, 1))
                    pe.wait_ge(s_vg, freed(a, 1))
                    for m in range(DC):
                        for c in range(DC):
                            pe.matmul(psK[:, m, 0:L], wa[:, c, m * P:(m + 1) * P], cx[:, ua, c, :],
                                      start=c == 0, stop=c == DC - 1)
                    for c in range(DC):
                        mm = pe.matmul(psV[0:L, 0:D], cx[:, ua, c, :], wc[:, c, :], start=c == 0, stop=c == DC - 1)
                    mm.then_inc(s_kv, 1)
                if here(o):
                    pe.wait_ge(s_en, done(o))
                    pe.wait_ge(s_eT, freed(o, 1))
                    for j in range(QT):
                        mm = pe.transpose(psET[0:L, j, 0:P], en[:, uo % 2, j, :], ident[:, :])
                    mm.then_inc(s_eTp, 1)
                if here(a):
                    pe.wait_ge(s_h, done(a))
                    pe.wait_ge(s_hT, freed(a, 1))
                    for j in range(QT):
                        for c in range(DC):
                            mm = pe.transpose(psHT[:, j, c, :], h[:, ua % 2, j, c * P:(c + 1) * P], ident[:, :])
                    mm.then_inc(s_hTp, 1)
                if here(h_):
                    pe.wait_ge(s_h2, done(h_))
                    pe.wait_ge(s_h2T, freed(h_, 1))
                    for j in range(QT):
                        for c in range(DC):
                            mm = pe.transpose(psH2T[:, j, c, :], xrow[:, uh, j, c * P:(c + 1) * P], ident[:, :])
                    mm.then_inc(s_h2Tp, 1)
                if here(r):
                    pe.wait_ge(s_occ, done(r))
                    pe.wait_ge(s_acc, freed(r, 1))
                    pe.matmul(pos[:, 0, :], tri[:, :], occ[:, 0, :], start=True, stop=False)
                    pe.matmul(pos[:, 0, :], ones[:, :], acc[:, :], start=False, stop=True)
                    pe.matmul(pos[:, 1, :], tri[:, :], occ[:, 1, :], start=True, stop=False)
                    pe.matmul(pos[:, 1, :], ones[:, :], occ[:, 0, :], start=False, stop=False)
                    pe.matmul(pos[:, 1, :], ones[:, :], acc[:, :], start=False, stop=True).then_inc(s_p, 1)
                if here(o):
                    pe.wait_ge(s_th, freed(o, 1))
                    for j in range(QT):
                        for c in range(DC):
                            pe.matmul(psO[:, j, :], hT[:, uo % 2, j, c, :], wc[:, DC + c, :], start=c == 0, stop=False)
                        if j == 0:
                            pe.wait_ge(s_eT, done(o))
                            pe.wait_ge(s_vg, done(o))
                        mm = pe.matmul(psO[:, j, :], eT[:, uo % 2, j, :], vg[:, uo % 2, :], start=False, stop=True)
                    mm.then_inc(s_o, 1)
                if here(a):
                    pe.wait_ge(s_hT, done(a))
                    pe.wait_ge(s_kn, done(a))
                    pe.wait_ge(s_t, freed(a, 1))
                    for j in range(QT):
                        for c in range(DC):
                            mm = pe.matmul(psS[:, j, 0:L], hT[:, ua % 2, j, c, :], kn[:, ua % 2, c, :],
                                           start=c == 0, stop=c == DC - 1)
                    mm.then_inc(s_s, 1)
                if here(h_):
                    pe.wait_ge(s_h2T, done(h_))
                    pe.wait_ge(s_pe, freed(h_, 1))
                    for j in range(QT):
                        for c in range(DC):
                            mm = pe.matmul(score[:, j, :], h2T[:, j, c, :], gw[:, c, :],
                                           start=c == 0, stop=c == DC - 1)
                    mm.then_inc(s_g, 1)

            phase1(pe, step)

            pe.wait_ge(s_acc, done(NB - 1))
            pe.wait_ge(s_pe, done(NB - 1))
            pe.matmul(total, ones[:, :], acc[:, :], start=True, stop=True).then_inc(s_tot, 1)
            pe.wait_ge(s_tab, 1)
            pe.wait_ge(s_late_lo, LATE)

            def base(b, column):
                return pe.value_load(tab[0:1, ds(b, 1), column:column + 1].rearrange("a b c -> a (b c)"),
                                     min_val=0, max_val=WALL - WE)

            def step2(i, u):
                j, uj = i - 1, (u - 1) % U
                k, uk = i - 2, (u - 2) % U
                if in_blocks(i):
                    pe.wait_ge(s_xb[u], landed(i, u, U))
                    pe.wait_ge(s_xlo, freed(i, 1))
                    for c in range(DC):
                        mm = pe.transpose(psX[:, c, :], xb[:, u, c * P:(c + 1) * P], ident[:, :])
                    mm.then_inc(s_xtp, 1)
                if in_blocks(k):
                    pe.wait_ge(s_hid, done(k))
                    pe.wait_ge(s_hlo, freed(k, 1))
                    for c in range(FC):
                        mm = pe.transpose(psHH[:, c, :], hid[:, c * P:(c + 1) * P], ident[:, :])
                    mm.then_inc(s_htp, 1)
                if in_blocks(j):
                    hi, lo = base(j, 1), base(j, 2)
                    pe.wait_ge(s_xlo, done(j))
                    for half, (dst, free, out) in enumerate(((psH1, s_sil, s_h1), (psH2, s_hid, s_hh))):
                        pe.wait_ge(free, freed(j, 1))
                        n = 0
                        for part, w in ((0, hi), (0, lo), (1, hi)):
                            for c in range(DC):
                                mm = pe.matmul(dst[:, :], xt2[:, uj % 2, part, c, :],
                                               wall[:, ds(w + (c * 2 * FH + half * FH), FH)],
                                               start=n == 0, stop=n == 3 * DC - 1)
                                n += 1
                        mm.then_inc(out, 1)
                if in_blocks(k):
                    hi, lo = base(k, 1), base(k, 2)
                    pe.wait_ge(s_yb, freed(k, 2))
                    pe.wait_ge(s_hhi, done(k))
                    n = 0
                    for part, w in ((0, hi), (0, lo), (1, hi)):
                        if part == 1:
                            pe.wait_ge(s_hlo, done(k))
                        for c in range(FC):
                            mm = pe.matmul(psY[:, uk % 2, 0:D], ht2[:, part, c, :],
                                           wall[:, ds(w + (W2OFF + c * D), D)],
                                           start=n == 0, stop=n == 3 * FC - 1)
                            n += 1
                    mm.then_inc(s_y, 1)

            phase2(pe, step2)


def kernel(x, ctx_1024, condB_pt, _lenS2, L0_xcond_W_a, L0_xcond_W_c, L0_ffn_w12, L0_ffn_w3, L0_ffn_gate_w):
    import numpy as np
    import concourse.bacc as bacc
    from concourse.bass_utils import run_bass_kernel_spmd

    def chunks(a):
        return a.reshape(-1, P, a.shape[-1]).transpose(1, 0, 2)

    x, cx, wa, wc = (np.asarray(v) for v in (x, ctx_1024, L0_xcond_W_a, L0_xcond_W_c))
    w12, w3, gw = (np.asarray(v) for v in (L0_ffn_w12, L0_ffn_w3, L0_ffn_gate_w))
    w = np.concatenate(
        [part for e in range(NE) for part in (chunks(w12[e].T).reshape(P, -1), chunks(w3[e].T).reshape(P, -1))], axis=1)
    arrays = {
        "x_in": x.reshape(TOK, D),
        "context": cx.transpose(2, 0, 1).reshape(DC, P, NB, L).transpose(1, 2, 0, 3),
        "position": np.asarray(condB_pt),
        "length": np.asarray(_lenS2),
        "w_a": chunks(wa.T),
        "w_c": chunks(wc.T),
        "w_experts": w,
        "w_router": chunks(gw.T),
    }
    arrays = {k: np.ascontiguousarray(v) for k, v in arrays.items()}
    nc = bacc.Bacc("TRN2", target_bir_lowering=False, num_devices=1, dynamic_dma_scratch_size=4096)
    args = [nc.dram_tensor(k, v.shape, mybir.dt.from_np(v.dtype), kind="ExternalInput").ap() for k, v in arrays.items()]
    out = nc.dram_tensor("out_rows", (TOK + P, D), F32, kind="ExternalOutput").ap()
    build(nc, *args, out)
    r = run_bass_kernel_spmd(nc, [arrays], core_ids=[0])
    return r.results[0]["out_rows"][0:TOK].reshape(NB, QT * P, D)
```

```python
import concourse.bass as bass
from concourse import mybir
from contextlib import ExitStack

F32 = mybir.dt.float32
F32R = mybir.dt.float32r
BF16 = mybir.dt.bfloat16
I32 = mybir.dt.int32
ACT = mybir.ActivationFunctionType
ALU = mybir.AluOpType
AX = mybir.AxisListType
ds = bass.ds

P = 128
NB = 16
QT = 2
D = 256
DC = D // P
L = 120
NE = 8
FH = 512
FC = FH // P
TOK = NB * QT * P
WINDOW, DEV_POW, MASKED, EPS = 16.0, 128.0, 1.0e9, 1.0e-5

META = D
IDCOL = META + NE
ROW = 272
CAP = TOK + P
XS_ROWS = NE * CAP + P
NBLK = 2 * TOK // P + NE - 1
TABW = 3
RT = 2 * QT

WE = DC * 2 * FH + FC * D
PC = 1024
EARLY = 6
LATE = NE - EARLY
EARLYP = EARLY * WE // PC
LATEP = LATE * WE // PC
POOLP = 2
WALL = 2 * NE * WE
LATE0 = 2 * EARLY * WE
W2OFF = 2 * DC * 2 * FH
BIG = 3.0e38

CREDIT = 4
U = 4
PEEL = 8


def done(n):
    return CREDIT + 1 + n


def freed(n, ring):
    return CREDIT + 1 + n - ring


def landed(n, u):
    return (n - u) * (16 // U) + 16


def landed_piece(n, u):
    return (n - u % 2) * 8 + 16


def settle(engine, sem):
    engine.sem_inc(sem, 1)


def link(engine, instruction, sem, value):
    instruction.then_inc(sem, 1)
    engine.wait_ge(sem, value)


def build(nc, x_d, ctx_d, cond_d, len_d, wa_d, wc_d, w_d, gate_d, out_d):
    xs = nc.dram_tensor("expert_rows", [XS_ROWS, ROW], F32, kind="Internal").ap()
    x_v = x_d.rearrange("(b j p) d -> p b j d", j=QT, p=P)
    out_v = out_d[0:TOK, :].rearrange("(b j p) d -> p b j d", j=QT, p=P)

    with ExitStack() as ctx:
        def sem(name):
            return ctx.enter_context(nc.semaphore(name))

        def place(stack):
            return lambda name, shape, dt=F32: stack.enter_context(nc.sbuf_tensor(name, shape, dt))

        sb = place(ctx)
        ident = sb("ident", [P, P])
        tail = sb("tail", [P, ROW])
        tab = sb("tab", [1, NBLK, TABW], I32)
        tailrow = sb("tailrow", [1, NE], I32)
        unused = sb("unused", [P, 1])

        with ExitStack() as two:
            sb = place(two)
            wall = sb("wall", [P, WALL], F32R)
            xb = sb("xb", [P, U, ROW])
            meta = sb("meta", [P, U, NE + 1])
            xt2 = sb("xt2", [P, 2, 2, DC, P], F32R)
            sil = sb("sil", [P, FH])
            hid = sb("hid", [P, FH])
            ht2 = sb("ht2", [P, 2, FC, P], F32R)
            yb = sb("yb", [P, 2, D])
        late = wall[:, LATE0:WALL].rearrange("p (q h c) -> p q h c", h=2, c=PC)
        late_raw = late[:, :, 1, :].bitcast(F32)

        with ExitStack() as one:
            sb = place(one)
            sb("early_parts", [P, LATE0])
            last_pieces = nc.sbuf_base + (2 * LATE * WE - 4 * PC) * 4
            h = sb("h", [P, 2, QT, D])
            hT = sb("hT", [P, 2, QT, DC, P])
            th = sb("th", [P, QT, D])
            cx = sb("cx", [P, U, DC, L])
            wa = sb("wa", [P, DC, D])
            wc = sb("wc", [P, 2 * DC, D])
            kn = sb("kn", [P, DC, L])
            vg = sb("vg", [L, 2, D])
            tS = sb("tS", [P, QT, L])
            ex = sb("ex", [P, QT, L])
            en = sb("en", [P, QT, L])
            eT = sb("eT", [L, QT, P])
            gauss = sb("gauss", [L, NB])
            gdev = sb("gdev", [L, NB])
            cond = sb("cond", [P, NB])
            leni = sb("leni", [P, NB], I32)
            lenf = sb("lenf", [P, NB])
            first = sb("first", [P, NB])
            last = sb("last", [P, NB])
            lidx = sb("lidx", [P, L])
            keep = sb("keep", [P, L])
            bias = sb("bias", [P, L])
            assert nc.sbuf_base <= last_pieces
        with ExitStack() as one:
            sb = place(one)
            sb("before_last", [P, WALL - 4 * PC])
            wst = sb("wst", [P, 2, PC])
            xt = sb("x", [P, U, QT, D])
            assert U * QT * D == 2 * PC

        with ExitStack() as one:
            sb = place(one)
            sb("all_parts", [P, WALL])
            h2T = sb("h2T", [P, QT, DC, P])
            xrow = sb("xrow", [P, U * QT, ROW])
            gw = sb("gw", [P, DC, NE])
            pcol = sb("pcol", [P, 1])
            tri = sb("tri", [P, P], BF16)
            ones = sb("ones", [P, P], BF16)
            tokid = sb("tokid", [P, NB * QT], I32)
            ecap = sb("ecap", [P, NE])
            rank8 = sb("rank8", [P, NE])
            tmin = sb("tmin", [P, QT])
            rsum = sb("rsum", [P, QT])
            rinv = sb("rinv", [P, QT])
            bst = sb("bst", [P, 4, 6])
            mv = sb("mv", [P, U, 4, 2])
            ve = sb("ve", [P, 4])
            rstd = sb("rstd", [P, U, 4])
            nmr = sb("nmr", [P, 2, 4])
            mhalf = sb("mhalf", [P, 4])
            sc = sb("sc", [P, RT, NE])
            m12 = sb("m12", [P, 2, RT])
            k12 = sb("k12", [P, 2, RT])
            dm = sb("dm", [P, RT])
            e2 = sb("e2", [P, RT])
            den = sb("den", [P, RT])
            p1 = sb("p1", [P, RT])
            rt = sb("rt", [P, RT, NE])
            rk = sb("rk", [P, RT, NE])
            oh = sb("oh", [P, 2, RT, NE])
            occ = sb("occ", [P, RT, NE], BF16)
            occs = sb("occs", [P, NE])
            acc = sb("acc", [P, NE], BF16)
            pe8 = sb("pe8", [P, RT, NE])
            q8 = sb("q8", [P, 2, RT, NE])
            idx = sb("idx", [P, 2, 2, RT], I32)
            cnt = sb("cnt", [1, NE])
            j128 = sb("j128", [1, TOK // P])
            nblk = sb("nblk", [1, NE])
            one8 = sb("one8", [1, NE])
            end8 = sb("end8", [1, NE])
            skip8 = sb("skip8", [1, NE])
            biota = sb("biota", [1, NBLK])
            eb = sb("eb", [1, NBLK])
            rowb = sb("rowb", [1, NBLK])
            past = sb("past", [1, NBLK, NE])
            prod = sb("prod", [1, NBLK, NE])
            gt = sb("gt", [1, NE, TOK // P])

        def bank(name, shape, stack):
            return stack.enter_context(nc.psum_tensor(name, shape, F32))

        with ExitStack() as one:
            psK = bank("psK", [P, DC, 256], one)
            psV = bank("psV", [P, 512], one)
            psHT = bank("psHT", [P, QT, DC, P], one)
            psSE = bank("psSE", [P, 4, P], one)
            psO = bank("psO", [P, QT, D], one)
            psH2T = bank("psH2T", [P, QT, DC, P], one)
            psR = bank("psR", [P, 512], one)
            psP = bank("psP", [P, 512], one)
        with ExitStack() as two:
            psX = bank("psX", [P, 4, P], two)
            psHH = bank("psHH", [P, FC, P], two)
            psH1 = bank("psH1", [P, FH], two)
            psH2 = bank("psH2", [P, FH], two)
            psY = bank("psY", [P, 2, 512], two)
        score = psR[:, 0:RT * NE].rearrange("p (j e) -> p j e", e=NE)
        pos = psP[:, 0:RT * NE].rearrange("p (j e) -> p j e", e=NE)
        total = psP[:, 256:256 + NE]

        s_pos = sem("s_pos")
        s_mat = sem("s_mat")
        s_gw = sem("s_gw")
        s_x = [sem(f"s_xin{i}") for i in range(U)]
        s_cx = [sem(f"s_cx{i}") for i in range(U)]
        s_w = [sem(f"s_w{i}") for i in range(2)]
        s_res = [sem(f"s_res{i}") for i in range(U)]
        s_fill = sem("s_fill")
        s_scat = [sem(f"s_scat{i}") for i in range(2)]
        s_late = [sem(f"s_late{i}") for i in range(LATEP)]
        s_xb = [sem(f"s_xb{i}") for i in range(U)]
        s_add = sem("s_add")
        s_settle_pool = sem("s_settle_pool")
        s_settle_dve = sem("s_settle_dve")
        s_iota = sem("s_iota")
        s_cst = sem("s_cst")
        s_mask = sem("s_mask")
        s_gdev = sem("s_gdev")
        s_gauss = sem("s_gauss")
        s_st1 = sem("s_st1")
        s_st2 = sem("s_st2")
        s_ve = sem("s_ve")
        s_rstd = sem("s_rstd")
        s_h = sem("s_h")
        s_hTp = sem("s_hTp")
        s_hT = sem("s_hT")
        s_k = sem("s_k")
        s_v = sem("s_v")
        s_ms = sem("s_ms")
        s_kn = sem("s_kn")
        s_vg = sem("s_vg")
        s_s = sem("s_s")
        s_t = sem("s_t")
        s_ex = sem("s_ex")
        s_ri = sem("s_ri")
        s_en = sem("s_en")
        s_eTp = sem("s_eTp")
        s_eT = sem("s_eT")
        s_o = sem("s_o")
        s_th = sem("s_th")
        s_x2 = sem("s_x2")
        s_nmr = sem("s_nmr")
        s_h2 = sem("s_h2")
        s_h2Tp = sem("s_h2Tp")
        s_h2T = sem("s_h2T")
        s_g = sem("s_g")
        s_sc = sem("s_sc")
        s_dm = sem("s_dm")
        s_e2 = sem("s_e2")
        s_occ = sem("s_occ")
        s_p = sem("s_p")
        s_pe = sem("s_pe")
        s_idx = sem("s_idx")
        s_acc = sem("s_acc")
        s_r = sem("s_r")
        s_q = sem("s_q")
        s_whi = sem("s_whi")
        s_wlo = sem("s_wlo")
        s_tot = sem("s_tot")
        s_tc = sem("s_tc")
        s_tailrow = sem("s_tailrow")
        s_tab = sem("s_tab")
        s_late_hi = sem("s_late_hi")
        s_late_lo = sem("s_late_lo")
        s_pool_lo = sem("s_pool_lo")
        s_xtp = sem("s_xtp")
        s_meta = sem("s_meta")
        s_xhi = sem("s_xhi")
        s_xlo = sem("s_xlo")
        s_h1 = sem("s_h1")
        s_hh = sem("s_hh")
        s_sil = sem("s_sil")
        s_hid = sem("s_hid")
        s_htp = sem("s_htp")
        s_hhi = sem("s_hhi")
        s_hlo = sem("s_hlo")
        s_y = sem("s_y")
        s_yb = sem("s_yb")
        R_OPS, Q_OPS = 11, 6

        block = ctx.enter_context(nc.Block())

        def start(engine, *sems):
            for s in sems:
                engine.sem_inc(s, CREDIT)

        STEPS1 = NB + 6

        def here(n):
            return not isinstance(n, int) or 0 <= n < NB

        def pair(s, u):
            return u % 2 == 1 and here(s - 5)

        def numbered(s, u):
            return u % 2 == 0 and here(s - 6)

        def pieces(s):
            return [s] if here(s) else list(range(NB, EARLYP)) if s == NB + 2 else []

        def phase1(engine, step):
            for s in range(PEEL):
                step(s, s % U)
            with engine.Fori(PEEL, NB - U + 1, U) as g:
                for u in range(U):
                    step(g + u, u)
            for s in range(NB, STEPS1):
                step(s, s % U)

        STEPS2 = NBLK + 2

        def exists(n):
            return not isinstance(n, int) or 0 <= n < NBLK

        def phase2(engine, step, peel):
            end = peel + (NBLK - peel) // U * U
            for i in range(peel):
                step(i, i % U)
            with engine.Fori(peel, end - U + 1, U) as g:
                for u in range(U):
                    step(g + u, (peel + u) % U)
            for i in range(end, STEPS2):
                step(i, i % U)

        def entry(b, column):
            return tab[0:1, ds(b, 1), column:column + 1].rearrange("a b c -> a (b c)")

        def fill(engine, experts):
            engine.wait_ge(s_tailrow, 1)
            for e in experts:
                r = engine.value_load(tailrow[0:1, e:e + 1], min_val=e * CAP, max_val=e * CAP + TOK)
                engine.dma_start(xs[ds(r, P), :], tail[:, :]).then_inc(s_fill, 16)

        @block.sync
        def _(sp):
            sp.dma_start(cond[:, :], cond_d.rearrange("(a n) -> a n", a=1).to_broadcast([P, NB])).then_inc(s_pos, 16)
            sp.dma_start(leni[:, :], len_d.rearrange("(a n) -> a n", a=1).to_broadcast([P, NB])).then_inc(s_pos, 16)

            def load(b, u):
                if not isinstance(b, int) or b >= U:
                    sp.wait_ge(s_res[u], 4 * (b - u))
                    sp.wait_ge(s_h2, freed(b, U))
                    sp.wait_ge(s_v, freed(b, U))
                sp.dma_start(xt[:, u, :, :], x_v[:, ds(b, 1), :, :].rearrange("p b j d -> p (b j) d")).then_inc(s_x[u], 16)
                sp.dma_start(cx[:, u, :, :], ctx_d[:, ds(b, 1), :, :].rearrange("p b c l -> p (b c) l")).then_inc(s_cx[u], 16)

            def load_piece(n, u):
                if not isinstance(n, int) or n >= 2:
                    sp.wait_ge(s_wlo, freed(n, 2))
                sp.dma_start(wst[:, u % 2, :], w_d[:, ds(n * PC, PC)]).then_inc(s_w[u % 2], 16)

            def store(b, u):
                sp.wait_ge(s_x2, done(b))
                sp.dma_start(out_v[:, ds(b, 1), :, :].rearrange("p b j d -> p (b j) d"), xt[:, u, :, :]).then_inc(s_res[u], 16)

            load(0, 0)
            sp.dma_start(wa[:, :, :], wa_d).then_inc(s_mat, 16)
            sp.dma_start(wc[:, :, :], wc_d).then_inc(s_mat, 16)
            load_piece(0, 0)
            load_piece(1, 1)
            sp.dma_start(gw[:, :, :], gate_d).then_inc(s_gw, 16)
            for b in range(1, U):
                load(b, b)
            load_piece(2, 0)
            load_piece(3, 1)
            with sp.Fori(U, NB - U + 1, U) as g:
                for u in range(U):
                    b = g + u
                    load_piece(b, u)
                    store(b - U, u)
                    load(b, u)
            for n in range(NB, EARLYP):
                load_piece(n, n)
            for b in range(NB - U, NB):
                store(b, b % U)

            def load_late(q):
                sp.dma_start(late_raw[:, q, :], w_d[:, EARLY * WE + q * PC:EARLY * WE + (q + 1) * PC]).then_inc(s_late[q], 16)

            load_late(0)
            sp.wait_ge(s_scat[1], 64 * (NB - U) // 2)
            for q in range(1, LATEP - 2):
                load_late(q)
            sp.wait_ge(s_wlo, done(EARLYP - 1))
            load_late(LATEP - 2)
            sp.wait_ge(s_h2, done(NB - 1))
            for u in range(U):
                sp.wait_ge(s_res[u], 16 * (NB // U))
            load_late(LATEP - 1)
            sp.dma_start(xs[NE * CAP:NE * CAP + P, :], tail[:, :]).then_inc(s_fill, 16)
            sp.dma_start(out_d[TOK:TOK + P, :], tail[:, 0:D]).then_inc(s_fill, 16)
            fill(sp, range(NE // 2))
            sp.wait_ge(s_tab, 1)

            def load_block(b, u):
                r = sp.value_load(entry(b, 0), min_val=0, max_val=NE * CAP)
                if isinstance(b, int) and b == 0:
                    sp.wait_ge(s_scat[0], 32 * NB)
                    sp.wait_ge(s_scat[1], 32 * NB)
                    sp.wait_ge(s_fill, 16 * (NE + 2))
                sp.wait_ge(s_xtp, freed(b, U))
                sp.wait_ge(s_meta, freed(b, U))
                sp.dma_start(xb[:, u, :], xs[ds(r, P), :]).then_inc(s_xb[u], 16)

            for b in range(U):
                load_block(b, b)
            with sp.Fori(U, NBLK // U * U - U + 1, U) as g:
                for u in range(U):
                    load_block(g + u, u)
            for b in range(NBLK // U * U, NBLK):
                load_block(b, b % U)
            sp.wait_ge(s_add, 16 * NBLK)

        @block.gpsimd
        def _(pool):
            start(pool, s_x2, s_rstd)
            n = 0

            def made(instruction):
                nonlocal n
                n += 1
                link(pool, instruction, s_iota, n)

            exact = dict(allow_small_or_imprecise_dtypes=True)
            pool.iota(lidx[:, :], pattern=[[1, L]], base=0, channel_multiplier=0, **exact)
            pool.memset(mhalf[:, :], -0.5)
            pool.memset(ident[:, :], 0.0).then_inc(s_cst, 1)
            pool.iota(pcol[:, :], pattern=[[0, 1]], base=0, channel_multiplier=1, **exact).then_inc(s_cst, 1)
            pool.wait_ge(s_cst, 1)
            pool.affine_select(out=ident[:, :], in_=ident[:, :], compare_op=ALU.not_equal, fill=1.0,
                               base=0, pattern=[[-1, P]], channel_multiplier=1).then_inc(s_cst, 1)

            def rest():
                made(pool.memset(ones[:, :], 1.0))
                pool.affine_select(out=tri[:, :], in_=ones[:, :], compare_op=ALU.is_gt, fill=0.0,
                                   base=0, pattern=[[1, P]], channel_multiplier=-1)
                pool.iota(tokid[:, :], pattern=[[P, NB * QT]], base=0, channel_multiplier=1)
                pool.iota(ecap[:, :], pattern=[[CAP, NE]], base=0, channel_multiplier=0, **exact)
                pool.iota(rank8[:, :], pattern=[[-1, NE]], base=NE, channel_multiplier=0, **exact)
                pool.iota(j128[:, :], pattern=[[P, TOK // P]], base=0, channel_multiplier=0, **exact)
                pool.iota(biota[:, :], pattern=[[1, NBLK]], base=0, channel_multiplier=0, **exact)
                pool.memset(one8[:, :], 1.0)
                pool.memset(acc[:, :], 0.0)
                pool.memset(xrow[:, :, META:ROW], 0.0)
                made(pool.memset(tail[:, :], 0.0))
                pool.iota(tail[:, IDCOL:IDCOL + 1].bitcast(I32), pattern=[[0, 1]], base=TOK,
                          channel_multiplier=1).then_inc(s_cst, 1)

            def step(s, u):
                o, uo = s - 2, (u - 2) % U
                h_ = s - 3
                c, uc = s - 6, (u - 6) % U

                def scatter(k, j):
                    tile = uc % 2 * QT + j
                    pool.indirect_dma_start(
                        xs, bass.IndirectOffsetOnAxis(ap=idx[:, uc // 2, k, tile:tile + 1], axis=0),
                        xrow[:, uc * QT + j, :], None).then_inc(s_scat[uc % 2], 16)

                def ready():
                    if not isinstance(c, int) or c > 1:
                        pool.wait_ge(s_scat[uc % 2], 32 * (c - uc % 2))
                    pool.wait_ge(s_idx, done(c))
                    settle(pool, s_settle_pool)

                if here(c) and u % 2 == 1:
                    ready()
                    scatter(0, 0)
                if isinstance(s, int) and s == STEPS1 - 2:
                    for q in range(POOLP):
                        pool.wait_ge(s_late_hi, q + 1)
                        pool.tensor_tensor(late[:, q, 1, :], late_raw[:, q, :], late[:, q, 0, :].bitcast(F32),
                                           ALU.subtract).then_inc(s_pool_lo, 1)
                lo, hi = (0 if here(s) else 2), (4 if here(h_) else 2)
                if lo < hi:
                    pool.wait_ge(s_ve, done(s))
                    pool.tensor_tensor(rstd[:, u, lo:hi], ve[:, lo:hi], mhalf[:, lo:hi], ALU.pow).then_inc(s_rstd, 1)
                if isinstance(s, int) and s == 0:
                    rest()
                if here(c) and u % 2 == 0:
                    ready()
                    scatter(0, 0)
                if here(c):
                    scatter(1, 0)
                if here(o):
                    pool.wait_ge(s_th, done(o))
                    pool.tensor_tensor(xt[:, uo, :, :], xt[:, uo, :, :], th[:, :, :], ALU.add).then_inc(s_x2, 1)
                if here(c):
                    scatter(0, 1)
                    scatter(1, 1)

            phase1(pool, step)

            def step2(i, u):
                k, uk = i - 2, (u - 2) % U
                if exists(k):
                    pool.wait_ge(s_yb, done(k))
                    if not isinstance(k, int) or k > 0:
                        pool.wait_ge(s_add, 16 * k)
                    settle(pool, s_settle_pool)
                    pool.indirect_dma_start(out_d, bass.IndirectOffsetOnAxis(ap=meta[:, uk, NE:NE + 1].bitcast(I32), axis=0),
                                            yb[:, uk % 2, :], None, compute_op=ALU.add).then_inc(s_add, 16)

            pool.wait_ge(s_fill, 16 * (NE + 2))
            for u in range(U):
                pool.wait_ge(s_res[u], 16 * (NB // U))
            phase2(pool, step2, 3)

        @block.scalar
        def _(act):
            start(act, s_h, s_vg, s_eT, s_hT, s_h2T, s_e2, s_whi, s_th, s_ex, s_h2, s_xhi, s_hhi, s_sil, s_yb)
            act.wait_ge(s_gdev, 2)
            act.activation(gauss[:, :], gdev[:, :], ACT.Exp, scale=-1.0 / DEV_POW).then_inc(s_gauss, 1)
            act.wait_ge(s_gauss, 1)

            def late_hi(pieces):
                for q in pieces:
                    act.wait_ge(s_late[q], 16)
                    act.activation(late[:, q, 0, :], late_raw[:, q, :], ACT.Copy).then_inc(s_late_hi, 1)

            def high(n, u):
                act.wait_ge(s_w[u % 2], landed_piece(n, u))
                act.activation(wall[:, ds(n * 2 * PC, PC)], wst[:, u % 2, :], ACT.Copy).then_inc(s_whi, 1)

            def step(s, u):
                a, ua = s - 1, (u - 1) % U
                o, uo = s - 2, (u - 2) % U
                h_, uh = s - 3, (u - 3) % U
                if isinstance(s, int) and s == NB + 3:
                    late_hi(range(LATEP // 2))
                if here(a):
                    act.wait_ge(s_nmr, done(a))
                    act.wait_ge(s_hTp, freed(a, 2))
                    for j in range(QT):
                        norm = act.activation(h[:, ua % 2, j, :], xt[:, ua, j, :], ACT.Identity,
                                              bias=nmr[:, ua % 2, j:j + 1], scale=rstd[:, ua, j:j + 1])
                    norm.then_inc(s_h, 1)
                if here(o):
                    act.wait_ge(s_eTp, done(o))
                    act.wait_ge(s_o, freed(o, 1))
                    act.activation(eT[:, :, :], psSE[0:L, 2:4, :], ACT.Copy).then_inc(s_eT, 1)
                for n in pieces(s)[:1]:
                    high(n, u)
                if here(a):
                    act.wait_ge(s_hTp, done(a))
                    act.wait_ge(s_o, freed(a, 2))
                    act.activation(hT[:, ua % 2, :, :, :], psHT[:, :, :, :], ACT.Copy).then_inc(s_hT, 1)
                if here(o):
                    act.wait_ge(s_o, done(o))
                    act.wait_ge(s_x2, freed(o, 1))
                    act.activation(th[:, :, :], psO[:, :, :], ACT.Tanh).then_inc(s_th, 1)

                def exponentials():
                    act.wait_ge(s_t, done(a))
                    act.wait_ge(s_en, freed(a, 1))
                    for j in range(QT):
                        e = act.activation(ex[:, j, :], tS[:, j, :], ACT.Exp, bias=tmin[:, j:j + 1], scale=-1.0,
                                           accum_out=rsum[:, j:j + 1])
                    e.then_inc(s_ex, 1)

                if here(a) and u % 2 == 1:
                    exponentials()
                if here(h_):
                    act.wait_ge(s_nmr, done(s))
                    if not isinstance(h_, int) or h_ >= U:
                        act.wait_ge(s_scat[uh % 2], 32 * (h_ - U - uh % 2) + 64)
                    for j in range(QT):
                        norm = act.activation(xrow[:, uh * QT + j, 0:D], xt[:, uh, j, :], ACT.Identity,
                                              bias=nmr[:, u % 2, 2 + j:3 + j], scale=rstd[:, u, 2 + j:3 + j])
                    norm.then_inc(s_h2, 1)
                if here(a) and u % 2 == 0:
                    exponentials()
                for n in pieces(s)[1:]:
                    high(n, u + 1)
                if pair(s, u):
                    act.wait_ge(s_dm, done(s - 4))
                    act.activation(e2[:, :], dm[:, :], ACT.Exp).then_inc(s_e2, 2)
                if here(s):
                    act.wait_ge(s_v, done(s))
                    act.wait_ge(s_o, freed(s, 2))
                    act.activation(vg[:, u % 2, :], psV[0:L, 0:D], ACT.Copy,
                                   scale=gauss[:, ds(s, 1)]).then_inc(s_vg, 1)
                if here(h_):
                    act.wait_ge(s_h2Tp, done(h_))
                    act.wait_ge(s_g, freed(h_, 1))
                    act.activation(h2T[:, :, :, :], psH2T[:, :, :, :], ACT.Copy).then_inc(s_h2T, 1)

            phase1(act, step)

            late_hi(range(LATEP // 2, LATEP))
            fill(act, range(NE // 2, NE))
            act.activation(unused[:, :], ident[:, 0:1], ACT.Silu)

            def step2(i, u):
                j, k, uk = i - 1, i - 2, (u - 2) % U
                if exists(i):
                    act.wait_ge(s_xtp, done(i))
                    act.wait_ge(s_hh, freed(i, 2))
                    act.activation(xt2[:, u % 2, 0, :, :], psX[:, 0:DC, :], ACT.Copy).then_inc(s_xhi, 1)
                if exists(k):
                    act.wait_ge(s_htp, done(k))
                    act.wait_ge(s_y, freed(k, 1))
                    act.activation(ht2[:, 0, :, :], psHH[:, :, :], ACT.Copy).then_inc(s_hhi, 1)
                if exists(j):
                    act.wait_ge(s_h1, done(j))
                    act.wait_ge(s_hid, freed(j, 1))
                    act.activation(sil[:, :], psH1[:, :], ACT.Silu).then_inc(s_sil, 1)
                if exists(k):
                    e = act.value_load(entry(k, 1), min_val=0, max_val=NE - 1)
                    act.wait_ge(s_y, done(k))
                    if not isinstance(k, int) or k > 1:
                        act.wait_ge(s_add, 16 * (k - 1))
                    act.activation(yb[:, uk % 2, :], psY[:, uk % 2, 0:D], ACT.Copy,
                                   scale=meta[:, uk, ds(e, 1)]).then_inc(s_yb, 1)

            phase2(act, step2, 4)

        @block.vector
        def _(dve):
            start(dve, s_kn, s_ve, s_t, s_en, s_nmr, s_occ, s_pe, s_idx, s_acc, s_sc, s_dm, s_wlo,
                  s_meta, s_xlo, s_hid, s_hlo)
            dve.wait_ge(s_pos, 32)
            dve.wait_ge(s_cst, 2)
            link(dve, dve.tensor_copy(lenf[:, :], leni[:, :]), s_mask, 1)
            dve.tensor_scalar(first[:, :], cond[:, :], -WINDOW, 0.0, ALU.add, ALU.max)
            link(dve, dve.tensor_scalar(last[:, :], cond[:, :], WINDOW, None, ALU.add), s_mask, 2)
            link(dve, dve.tensor_tensor(last[:, :], last[:, :], lenf[:, :], ALU.min), s_mask, 3)
            link(dve, dve.tensor_scalar(gdev[:, :], cond[0:L, :], pcol[0:L, 0:1], None, ALU.subtract), s_gdev, 1)
            dve.tensor_tensor(gdev[:, :], gdev[:, :], gdev[:, :], ALU.mult).then_inc(s_gdev, 1)

            d8 = rank8[:, :].unsqueeze(1).to_broadcast([P, RT, NE])

            def wide(v):
                return v.unsqueeze(2).to_broadcast([P, RT, NE])

            def low(n, u):
                dve.wait_ge(s_whi, done(n))
                dve.tensor_tensor(wall[:, ds(n * 2 * PC + PC, PC)], wst[:, u % 2, :],
                                  wall[:, ds(n * 2 * PC, PC)].bitcast(F32), ALU.subtract).then_inc(s_wlo, 1)

            def step(s, u):
                a = s - 1
                h_, uh = s - 3, (u - 3) % U
                route = pair(s, u)

                def r_after(n):
                    dve.wait_ge(s_r, R_OPS * (s - 5) + 2 * n)

                def q_after(n, r0):
                    dve.wait_ge(s_q, Q_OPS * r0 + 2 * n)

                if here(h_):
                    dve.wait_ge(s_x2, done(h_))
                    dve.bn_stats(bst[:, 2, :], xt[:, uh, 0, :]).then_inc(s_st2, 1)
                    dve.bn_stats(bst[:, 3, :], xt[:, uh, 1, :]).then_inc(s_st2, 1)
                if here(s):
                    dve.wait_ge(s_x[u], landed(s, u))
                    dve.bn_stats(bst[:, 0, :], xt[:, u, 0, :]).then_inc(s_st1, 1)
                    dve.bn_stats(bst[:, 1, :], xt[:, u, 1, :]).then_inc(s_st1, 1)
                if here(h_):
                    dve.wait_ge(s_st2, 4 * h_ + 2)
                    settle(dve, s_settle_dve)
                    dve.bn_aggr(mv[:, u, 2, :], bst[:, 2, :]).then_inc(s_st2, 1)
                    dve.bn_aggr(mv[:, u, 3, :], bst[:, 3, :]).then_inc(s_st2, 1)
                if route:
                    if isinstance(s, int) and s == 5:
                        dve.wait_ge(s_cst, 4)
                    dve.wait_ge(s_g, done(s - 4))
                    dve.tensor_copy(sc[:, :, :], score).then_inc(s_sc, 2)
                if numbered(s, u):
                    dve.wait_ge(s_p, done(s - 5))
                    dve.tensor_tensor(pe8[:, :, :], pos, ecap[:, :].unsqueeze(1).to_broadcast([P, RT, NE]),
                                      ALU.add).then_inc(s_pe, 2)
                if here(s):
                    dve.wait_ge(s_st1, 4 * s + 2)
                    settle(dve, s_settle_dve)
                    dve.bn_aggr(mv[:, u, 0, :], bst[:, 0, :]).then_inc(s_st1, 1)
                    dve.bn_aggr(mv[:, u, 1, :], bst[:, 1, :]).then_inc(s_st1, 1)
                if numbered(s, u):
                    dve.wait_ge(s_pe, done(s - 5))
                    dve.tensor_tensor(q8[:, :, :, :], oh[:, :, :, :],
                                      pe8[:, :, :].unsqueeze(1).to_broadcast([P, 2, RT, NE]), ALU.mult).then_inc(s_q, 2)
                if route:
                    dve.wait_ge(s_sc, done(s - 4))
                    dve.tensor_reduce(m12[:, 0, :], sc[:, :, :], AX.X, ALU.max).then_inc(s_r, 2)
                lo, hi = (0 if here(s) else 2), (4 if here(h_) else 2)
                if lo < hi:
                    if here(h_):
                        dve.wait_ge(s_st2, 4 * h_ + 4)
                    if here(s):
                        dve.wait_ge(s_st1, 4 * s + 4)
                    dve.wait_ge(s_rstd, done(s - 1))
                    dve.tensor_scalar(ve[:, lo:hi], mv[:, u, lo:hi, 1:2].rearrange("p a b -> p (a b)"),
                                      EPS, None, ALU.add).then_inc(s_ve, 1)
                if route:
                    r_after(1)
                    dve.tensor_tensor(rt[:, :, :], sc[:, :, :], wide(m12[:, 0, :]), ALU.is_equal).then_inc(s_r, 2)
                if here(s):
                    dve.tensor_scalar(keep[:, :], lidx[:, :], first[:, ds(s, 1)], -1.0,
                                      ALU.is_ge, ALU.mult).then_inc(s_ms, 1)
                if route:
                    r_after(2)
                    dve.tensor_tensor(rk[:, :, :], rt[:, :, :], d8, ALU.mult).then_inc(s_r, 2)
                if numbered(s, u):
                    q_after(6, s - 6)
                    with nc.allow_low_precision(reason="sums of whole numbers below 2**24 are exact"):
                        dve.tensor_reduce(idx[:, (u - 6) % U // 2, :, :], q8[:, :, :, :], AX.X, ALU.add).then_inc(s_idx, 2)
                    q_after(5, s - 6)
                    dve.tensor_tensor(acc[:, :], acc[:, :], occs[:, :], ALU.add).then_inc(s_acc, 2)
                if here(s):
                    dve.wait_ge(s_ms, 3 * s + 1)
                    dve.scalar_tensor_tensor(out=keep[:, :], in0=lidx[:, :], scalar=last[:, ds(s, 1)], in1=keep[:, :],
                                             op0=ALU.is_le, op1=ALU.mult).then_inc(s_ms, 1)
                if route:
                    r_after(3)
                    dve.tensor_reduce(k12[:, 0, :], rk[:, :, :], AX.X, ALU.max).then_inc(s_r, 2)
                if lo < hi:
                    dve.wait_ge(s_rstd, done(s))
                    dve.scalar_tensor_tensor(out=nmr[:, u % 2, lo:hi], in0=mv[:, u, lo:hi, 0:1].rearrange("p a b -> p (a b)"),
                                             scalar=-1.0, in1=rstd[:, u, lo:hi], op0=ALU.mult, op1=ALU.mult).then_inc(s_nmr, 1)
                if route:
                    r_after(4)
                    dve.tensor_tensor(oh[:, 0, :, :], d8, wide(k12[:, 0, :]), ALU.is_equal).then_inc(s_r, 2)
                if here(a):
                    dve.wait_ge(s_s, done(a))
                    dve.wait_ge(s_ms, 3 * a + 3)
                    settle(dve, s_settle_dve)
                    for j in range(QT):
                        t = dve.tensor_tensor_reduce(out=tS[:, j, :], in0=psSE[:, j, 0:L], in1=bias[:, :],
                                                     scale=1.0, scalar=BIG, op0=ALU.add, op1=ALU.min,
                                                     accum_out=tmin[:, j:j + 1])
                    t.then_inc(s_t, 1)
                if route:
                    r_after(5)
                    dve.scalar_tensor_tensor(out=rt[:, :, :], in0=oh[:, 0, :, :], scalar=-BIG, in1=sc[:, :, :],
                                             op0=ALU.mult, op1=ALU.add).then_inc(s_r, 2)
                for n in pieces(s)[:1]:
                    low(n, u)
                if route:
                    r_after(6)
                    dve.tensor_reduce(m12[:, 1, :], rt[:, :, :], AX.X, ALU.max).then_inc(s_r, 2)
                    r_after(7)
                    dve.wait_ge(s_e2, done(s - 6))
                    dve.tensor_tensor(dm[:, :], m12[:, 1, :], m12[:, 0, :], ALU.subtract).then_inc(s_dm, 2)
                    dve.tensor_tensor(rk[:, :, :], rt[:, :, :], wide(m12[:, 1, :]), ALU.is_equal).then_inc(s_r, 2)
                    r_after(8)
                    dve.tensor_tensor(rt[:, :, :], rk[:, :, :], d8, ALU.mult).then_inc(s_r, 2)
                    r_after(9)
                    dve.tensor_reduce(k12[:, 1, :], rt[:, :, :], AX.X, ALU.max).then_inc(s_r, 2)
                if here(a):
                    dve.wait_ge(s_ex, done(a))
                    dve.reciprocal(rinv[:, :], rsum[:, :]).then_inc(s_ri, 1)
                if route:
                    r_after(10)
                    dve.tensor_tensor(oh[:, 1, :, :], d8, wide(k12[:, 1, :]), ALU.is_equal).then_inc(s_r, 2)
                if here(a):
                    dve.wait_ge(s_ri, a + 1)
                    dve.wait_ge(s_eTp, freed(a, 1))
                    dve.tensor_tensor(en[:, :, :], ex[:, :, :], rinv[:, :].unsqueeze(2).to_broadcast([P, QT, L]),
                                      ALU.mult).then_inc(s_en, 1)
                if route:
                    r_after(11)
                    dve.tensor_tensor(occ[:, :, :], oh[:, 0, :, :], oh[:, 1, :, :], ALU.add).then_inc(s_occ, 2)
                if here(s):
                    dve.wait_ge(s_ms, 3 * s + 2)
                    dve.wait_ge(s_k, done(s))
                    dve.wait_ge(s_s, freed(s, 1))
                    dve.tensor_tensor(kn[:, :, :], psK[:, :, 0:L],
                                      keep[:, :].unsqueeze(1).to_broadcast([P, DC, L]), ALU.mult).then_inc(s_kn, 1)
                    dve.wait_ge(s_t, done(a))
                    dve.tensor_scalar(bias[:, :], keep[:, :], MASKED, MASKED, ALU.mult, ALU.add).then_inc(s_ms, 1)
                if route:
                    dve.wait_ge(s_e2, done(s - 4))
                    dve.tensor_scalar(den[:, :], e2[:, :], 1.0, None, ALU.add).then_inc(s_q, 2)
                    dve.tensor_tensor(rt[:, :, :], oh[:, 1, :, :], wide(e2[:, :]), ALU.mult).then_inc(s_q, 2)
                    q_after(1, s - 5)
                    dve.reciprocal(p1[:, :], den[:, :]).then_inc(s_q, 2)
                    q_after(2, s - 5)
                    dve.tensor_tensor(rk[:, :, :], rt[:, :, :], oh[:, 0, :, :], ALU.add).then_inc(s_q, 2)
                    dve.wait_ge(s_occ, done(s - 4))
                    dve.tensor_reduce(occs[:, :], occ[:, :, :].rearrange("p j e -> p e j"), AX.X, ALU.add).then_inc(s_q, 2)
                    dve.tensor_copy(xrow[:, (u - 5) % U * QT:(u - 5) % U * QT + RT, IDCOL:IDCOL + 1].bitcast(I32),
                                    tokid[:, ds(QT * (s - 5), RT)].unsqueeze(2))
                    q_after(4, s - 5)
                    dve.tensor_tensor(xrow[:, (u - 5) % U * QT:(u - 5) % U * QT + RT, META:META + NE], rk[:, :, :],
                                      wide(p1[:, :]), ALU.mult)
                for n in pieces(s)[1:]:
                    low(n, u + 1)

            phase1(dve, step)

            q = 0

            def t(instruction):
                nonlocal q
                q += 1
                link(dve, instruction, s_tc, q)

            dve.wait_ge(s_tot, 1)
            t(dve.tensor_copy(cnt[:, :], total[0:1, :]))
            dve.tensor_tensor(tailrow[:, :], cnt[:, :], ecap[0:1, :], ALU.add).then_inc(s_tailrow, 1)
            NJ = TOK // P
            t(dve.tensor_tensor(gt[:, :, :], cnt[:, :].unsqueeze(2).to_broadcast([1, NE, NJ]),
                                j128[:, :].unsqueeze(1).to_broadcast([1, NE, NJ]), ALU.is_gt))
            t(dve.tensor_reduce(nblk[:, :], gt[:, :, :], AX.X, ALU.add))
            t(dve.tensor_tensor_scan(end8[:, :], one8[:, :], nblk[:, :], initial=0.0, op0=ALU.mult, op1=ALU.add))
            t(dve.tensor_tensor(past[:, :, :], biota[:, :].unsqueeze(2).to_broadcast([1, NBLK, NE]),
                                end8[:, :].unsqueeze(1).to_broadcast([1, NBLK, NE]), ALU.is_ge))
            t(dve.tensor_scalar(skip8[:, :], nblk[:, :], -float(P), float(CAP), ALU.mult, ALU.add))
            t(dve.tensor_tensor(prod[:, :, :], past[:, :, :],
                                skip8[:, :].unsqueeze(1).to_broadcast([1, NBLK, NE]), ALU.mult))
            t(dve.tensor_reduce(eb[:, :], past[:, :, :], AX.X, ALU.add))
            t(dve.tensor_reduce(rowb[:, :], prod[:, :, :], AX.X, ALU.add))

            def column(c):
                return tab[:, :, c:c + 1].rearrange("a b c -> a (b c)")

            t(dve.tensor_scalar(eb[:, :], eb[:, :], float(NE - 1), None, ALU.min))
            t(dve.scalar_tensor_tensor(out=rowb[:, :], in0=biota[:, :], scalar=float(P), in1=rowb[:, :],
                                       op0=ALU.mult, op1=ALU.add))
            dve.tensor_copy(column(1), eb[:, :])
            dve.tensor_scalar(column(2), eb[:, :], float(2 * WE), None, ALU.mult)
            dve.tensor_scalar(column(0), rowb[:, :], float(NE * CAP), None, ALU.min).then_inc(s_tab, 1)

            for q in range(POOLP, LATEP):
                dve.wait_ge(s_late_hi, q + 1)
                dve.tensor_tensor(late[:, q, 1, :], late_raw[:, q, :], late[:, q, 0, :].bitcast(F32),
                                  ALU.subtract).then_inc(s_late_lo, 1)

            def step2(i, u):
                j, k = i - 1, i - 2
                if exists(i):
                    dve.wait_ge(s_xb[u], landed(i, u))
                    if not isinstance(i, int) or i >= U:
                        dve.wait_ge(s_add, 16 * (i - U + 1))
                    dve.tensor_copy(meta[:, u, :], xb[:, u, META:IDCOL + 1]).then_inc(s_meta, 1)
                    dve.wait_ge(s_xhi, done(i))
                    dve.tensor_tensor(xt2[:, u % 2, 1, :, :], psX[:, 0:DC, :], xt2[:, u % 2, 0, :, :].bitcast(F32),
                                      ALU.subtract).then_inc(s_xlo, 1)
                if exists(k):
                    dve.wait_ge(s_hhi, done(k))
                    dve.tensor_tensor(ht2[:, 1, :, :], psHH[:, :, :], ht2[:, 0, :, :].bitcast(F32),
                                      ALU.subtract).then_inc(s_hlo, 1)
                if exists(j):
                    dve.wait_ge(s_sil, done(j))
                    dve.wait_ge(s_hh, done(j))
                    dve.wait_ge(s_htp, freed(j, 1))
                    dve.tensor_tensor(hid[:, :], sil[:, :], psH2[:, :], ALU.mult).then_inc(s_hid, 1)

            phase2(dve, step2, 4)

        @block.tensor
        def _(pe):
            start(pe, s_k, s_v, s_eTp, s_hTp, s_h2Tp, s_o, s_p, s_s, s_g, s_xtp, s_htp, s_h1, s_hh, s_y)
            pe.wait_ge(s_mat, 32)
            pe.wait_ge(s_cst, 3)
            pe.wait_ge(s_gauss, 1)

            def step(s, u):
                a, ua = s - 1, (u - 1) % U
                o, uo = s - 2, (u - 2) % U
                h_, uh = s - 3, (u - 3) % U
                g_, ug = s - 4, (u - 4) % U

                def old_rows(j):
                    for c in range(DC):
                        pe.matmul(psO[:, j, :], hT[:, uo % 2, j, c, :], wc[:, DC + c, :], start=c == 0, stop=False)

                if here(o):
                    pe.wait_ge(s_th, freed(o, 1))
                    old_rows(0)
                    pe.wait_ge(s_en, done(o))
                    for j in range(QT):
                        mm = pe.transpose(psSE[0:L, 2 + j, :], en[:, j, :], ident[:, :])
                    mm.then_inc(s_eTp, 1)
                if numbered(s, u):
                    pe.wait_ge(s_occ, done(s - 5))
                    pe.wait_ge(s_acc, done(s - 7))
                    pe.matmul(pos, tri[:, :], occ[:, :, :], start=True, stop=False)
                    for j in range(RT - 1):
                        pe.matmul(pos[:, j + 1:RT, :], ones[:, :], occ[:, j:j + 1, :].to_broadcast([P, RT - 1 - j, NE]),
                                  start=False, stop=False)
                    pe.matmul(pos, ones[:, :], acc[:, :].unsqueeze(1).to_broadcast([P, RT, NE]),
                              start=False, stop=True).then_inc(s_p, 2)
                if here(g_):
                    pe.wait_ge(s_h2T, done(g_))
                    if isinstance(g_, int) and g_ == 0:
                        pe.wait_ge(s_gw, 16)
                    if ug % 2 == 0:
                        pe.wait_ge(s_sc, done(s - 5))
                    for j in range(QT):
                        for c in range(DC):
                            mm = pe.matmul(score[:, ug % 2 * QT + j, :], h2T[:, j, c, :], gw[:, c, :],
                                           start=c == 0, stop=c == DC - 1)
                    mm.then_inc(s_g, 1)
                if here(a):
                    pe.wait_ge(s_h, done(a))
                    pe.wait_ge(s_hT, freed(a, 1))
                    for j in range(QT):
                        for c in range(DC):
                            mm = pe.transpose(psHT[:, j, c, :], h[:, ua % 2, j, c * P:(c + 1) * P], ident[:, :])
                    mm.then_inc(s_hTp, 1)
                if here(o):
                    pe.wait_ge(s_eT, done(o))
                    pe.matmul(psO[:, 0, :], eT[:, 0, :], vg[:, uo % 2, :], start=False, stop=True)
                    old_rows(1)
                    pe.matmul(psO[:, 1, :], eT[:, 1, :], vg[:, uo % 2, :], start=False, stop=True).then_inc(s_o, 1)
                if here(a):
                    pe.wait_ge(s_hT, done(a))
                    pe.wait_ge(s_kn, done(a))
                    for j in range(QT):
                        for c in range(DC):
                            mm = pe.matmul(psSE[:, j, 0:L], hT[:, ua % 2, j, c, :], kn[:, c, :],
                                           start=c == 0, stop=c == DC - 1)
                    mm.then_inc(s_s, 1)
                if here(s):
                    pe.wait_ge(s_cx[u], landed(s, u))
                    pe.wait_ge(s_kn, freed(s, 1))
                    for m in range(DC):
                        for c in range(DC):
                            mm = pe.matmul(psK[:, m, 0:L], wa[:, c, m * P:(m + 1) * P], cx[:, u, c, :],
                                           start=c == 0, stop=c == DC - 1)
                    mm.then_inc(s_k, 1)
                    pe.wait_ge(s_vg, freed(s, 1))
                    for c in range(DC):
                        mm = pe.matmul(psV[0:L, 0:D], cx[:, u, c, :], wc[:, c, :], start=c == 0, stop=c == DC - 1)
                    mm.then_inc(s_v, 1)
                if here(h_):
                    pe.wait_ge(s_h2, done(h_))
                    pe.wait_ge(s_h2T, freed(h_, 1))
                    for j in range(QT):
                        for c in range(DC):
                            mm = pe.transpose(psH2T[:, j, c, :], xrow[:, uh * QT + j, c * P:(c + 1) * P], ident[:, :])
                    mm.then_inc(s_h2Tp, 1)

            phase1(pe, step)

            pe.wait_ge(s_acc, done(NB - 1))
            pe.matmul(total, ones[:, :], acc[:, :], start=True, stop=True).then_inc(s_tot, 1)
            pe.wait_ge(s_tab, 1)
            at_w12, at_w3, at_next = (pe.alloc_register(n) for n in ("at_w12", "at_w3", "at_next"))
            pe.reg_mov(at_w12, 0)
            pe.reg_mov(at_w3, 0)
            pe.reg_mov(at_next, 0)

            def step2(i, u):
                j, uj = i - 1, (u - 1) % U
                k, uk = i - 2, (u - 2) % U
                limit = dict(min_val=0, max_val=2 * (NE - 1) * WE)
                if exists(i):
                    pe.wait_ge(s_xb[u], landed(i, u))
                    pe.wait_ge(s_xlo, freed(i, 1))
                    for c in range(DC):
                        mm = pe.transpose(psX[:, c, :], xb[:, u, c * P:(c + 1) * P], ident[:, :])
                    mm.then_inc(s_xtp, 1)
                if exists(k):
                    pe.wait_ge(s_hid, done(k))
                    pe.wait_ge(s_hlo, freed(k, 1))
                    for c in range(FC):
                        mm = pe.transpose(psHH[:, c, :], hid[:, c * P:(c + 1) * P], ident[:, :])
                    mm.then_inc(s_htp, 1)
                if exists(j):
                    if isinstance(j, int) and j == 0:
                        pe.wait_ge(s_late_lo, LATEP - POOLP)
                        pe.wait_ge(s_pool_lo, POOLP)
                    w = pe.snap(at_w12, **limit)
                    pe.wait_ge(s_xlo, done(j))
                    for half, (dst, free, out) in enumerate(((psH1, s_sil, s_h1), (psH2, s_hid, s_hh))):
                        pe.wait_ge(free, freed(j, 1))
                        n = 0
                        for xpart, wpart in ((0, 0), (0, 1), (1, 0)):
                            for c in range(DC):
                                mm = pe.matmul(dst[:, :], xt2[:, uj % 2, xpart, c, :],
                                               wall[:, ds(w + ((2 * c + wpart) * PC + half * FH), FH)],
                                               start=n == 0, stop=n == 3 * DC - 1)
                                n += 1
                        mm.then_inc(out, 1)
                if exists(i):
                    pe.reg_load(at_next, entry(i, 2))
                if exists(k):
                    w = pe.snap(at_w3, **limit)
                    pe.wait_ge(s_yb, freed(k, 2))
                    pe.wait_ge(s_hhi, done(k))
                    n = 0
                    for hpart, wpart in ((0, 0), (0, 1), (1, 0)):
                        if hpart == 1:
                            pe.wait_ge(s_hlo, done(k))
                        for c in range(FC):
                            mm = pe.matmul(psY[:, uk % 2, 0:D], ht2[:, hpart, c, :],
                                           wall[:, ds(w + (W2OFF + wpart * PC + c * D), D)],
                                           start=n == 0, stop=n == 3 * FC - 1)
                            n += 1
                    mm.then_inc(s_y, 1)
                pe.reg_mov(at_w3, at_w12)
                pe.reg_mov(at_w12, at_next)

            phase2(pe, step2, 2)


def kernel(x, ctx_1024, condB_pt, _lenS2, L0_xcond_W_a, L0_xcond_W_c, L0_ffn_w12, L0_ffn_w3, L0_ffn_gate_w):
    import numpy as np
    import concourse.bacc as bacc
    from concourse.bass_utils import run_bass_kernel_spmd

    def chunks(a):
        return a.reshape(-1, P, a.shape[-1]).transpose(1, 0, 2)

    x, cx, wa, wc = (np.asarray(v) for v in (x, ctx_1024, L0_xcond_W_a, L0_xcond_W_c))
    w12, w3, gw = (np.asarray(v) for v in (L0_ffn_w12, L0_ffn_w3, L0_ffn_gate_w))
    w = np.concatenate(
        [part for e in range(NE) for part in (chunks(w12[e].T).reshape(P, -1), chunks(w3[e].T).reshape(P, -1))], axis=1)
    arrays = {
        "x_in": x.reshape(TOK, D),
        "context": cx.transpose(2, 0, 1).reshape(DC, P, NB, L).transpose(1, 2, 0, 3),
        "position": np.asarray(condB_pt),
        "length": np.asarray(_lenS2),
        "w_a": chunks(wa.T),
        "w_c": chunks(wc.T),
        "w_experts": w,
        "w_router": chunks(gw.T),
    }
    arrays = {k: np.ascontiguousarray(v) for k, v in arrays.items()}
    nc = bacc.Bacc("TRN2", target_bir_lowering=False, num_devices=1, dynamic_dma_scratch_size=4096)
    args = [nc.dram_tensor(k, v.shape, mybir.dt.from_np(v.dtype), kind="ExternalInput").ap() for k, v in arrays.items()]
    out = nc.dram_tensor("out_rows", (TOK + P, D), F32, kind="ExternalOutput").ap()
    build(nc, *args, out)
    r = run_bass_kernel_spmd(nc, [arrays], core_ids=[0])
    return r.results[0]["out_rows"][0:TOK].reshape(NB, QT * P, D)
```
